# Optimizing a Trainium2 kernel written in Bass

```python
import numpy as np
import jax
import jax.numpy as jnp

def _softmax(x, axis=-1):
    return jax.nn.softmax(x, axis=axis)

def _gelu(x):
    return jax.nn.gelu(x, approximate=True)

def _silu(x):
    return jax.nn.silu(x)

def _sigmoid(x):
    return jax.nn.sigmoid(x)

def _layernorm(x, axis=-1, eps=1e-05):
    m = jnp.mean(x, axis=axis, keepdims=True)
    v = jnp.var(x, axis=axis, keepdims=True)
    return (x - m) / jnp.sqrt(v + eps)

def _scatter_add(tgt, idx, src, axis=0):
    return tgt.at[idx].add(src)

def _segment_sum(src, seg, n):
    return jax.ops.segment_sum(src, seg, n)
kernel_name = 'mk_gnn_resnorm_d2_gnn_r16_9d10c2'

def setup_inputs(seed: int=0):
    np.random.seed(seed)
    _w = jnp.asarray

    def _rec_inputs():
        import jax
        import jax.numpy as jnp
        _gk = jax.random.key(seed)
        x = -0.0002117 + 1 * jax.random.normal(jax.random.fold_in(_gk, 1), (6250, 256), jnp.float32)
        _s = jax.random.randint(jax.random.fold_in(_gk, 2), (50000,), 0, 6250, jnp.int32)
        _d = jax.random.randint(jax.random.fold_in(_gk, 3), (50000,), 0, 6250, jnp.int32)
        _loop = jnp.arange(6250, dtype=jnp.int32)
        src = jnp.concatenate([_s, _d, _loop])
        dst = jnp.concatenate([_d, _s, _loop])
        _o = jnp.argsort(dst, stable=True)
        src = src[_o]
        dst = dst[_o]
        return (x, src, dst)
    x, src, dst = _rec_inputs()

    def _L0_gnn_setup():
        import jax, jax.numpy as jnp
        import numpy as np
        N_NODES = 6250
        N_EDGES = 20000
        D_IN, D_HID, D_OUT = (256, 1024, 256)
        BN_EPS = 1e-05
        key = jax.random.key(seed)
        ks = jax.random.split(key, 6)
        x = jax.random.normal(ks[0], (N_NODES, D_IN), dtype=jnp.float32)
        edge_index = jax.random.randint(ks[1], (2, N_EDGES), 0, N_NODES, dtype=jnp.int64)
        W1 = jax.random.normal(ks[2], (D_IN, D_HID), dtype=jnp.float32) * (1.0 / np.sqrt(D_IN))
        b1 = jnp.zeros((D_HID,), dtype=jnp.float32)
        gamma = jnp.ones((D_HID,), dtype=jnp.float32)
        beta = jnp.zeros((D_HID,), dtype=jnp.float32)
        W2 = jax.random.normal(ks[3], (D_HID, D_OUT), dtype=jnp.float32) * (1.0 / np.sqrt(D_HID))
        b2 = jnp.zeros((D_OUT,), dtype=jnp.float32)
        return {'x': x, 'edge_index': edge_index, 'W1': W1, 'b1': b1, 'gamma': gamma, 'beta': beta, 'W2': W2, 'b2': b2}
    _L0_gnn_all = _L0_gnn_setup()
    _L0_gnn_in = {k: v for k, v in _L0_gnn_all.items() if k in ('W1', 'b1', 'gamma', 'beta', 'W2', 'b2')}
    del _L0_gnn_all

    def _L1_gnn_setup():
        import jax, jax.numpy as jnp
        import numpy as np
        N, E, D, H = (625, 20000, 256, 256)
        key = jax.random.key(seed)
        ks = jax.random.split(key, 8)
        s = 1.0 / np.sqrt(D)
        return {'x': jax.random.normal(ks[0], (N, D), jnp.float32), 'edge_index': jax.random.randint(ks[1], (2, E), 0, N, dtype=jnp.int32), 'W1': jax.random.normal(ks[2], (H, D), jnp.float32) * s, 'b1': jnp.zeros((H,), jnp.float32), 'W2': jax.random.normal(ks[3], (H, H), jnp.float32) * s, 'b2': jnp.zeros((H,), jnp.float32), 'W3': jax.random.normal(ks[4], (H, H), jnp.float32) * s, 'b3': jnp.zeros((H,), jnp.float32)}
    _L1_gnn_all = _L1_gnn_setup()
    _L1_gnn_in = {k: v for k, v in _L1_gnn_all.items() if k in ('W1', 'b1', 'W2', 'b2', 'W3', 'b3')}
    del _L1_gnn_all
    return {'x': x, 'src': src, 'dst': dst, 'L0_gnn_W1': _L0_gnn_in['W1'], 'L0_gnn_b1': _L0_gnn_in['b1'], 'L0_gnn_gamma': _L0_gnn_in['gamma'], 'L0_gnn_beta': _L0_gnn_in['beta'], 'L0_gnn_W2': _L0_gnn_in['W2'], 'L0_gnn_b2': _L0_gnn_in['b2'], 'L1_gnn_W1': _L1_gnn_in['W1'], 'L1_gnn_b1': _L1_gnn_in['b1'], 'L1_gnn_W2': _L1_gnn_in['W2'], 'L1_gnn_b2': _L1_gnn_in['b2'], 'L1_gnn_W3': _L1_gnn_in['W3'], 'L1_gnn_b3': _L1_gnn_in['b3']}

def reference(x, src, dst, L0_gnn_W1, L0_gnn_b1, L0_gnn_gamma, L0_gnn_beta, L0_gnn_W2, L0_gnn_b2, L1_gnn_W1, L1_gnn_b1, L1_gnn_W2, L1_gnn_b2, L1_gnn_W3, L1_gnn_b3):
    import jax
    import jax.numpy as jnp

    def _L0_gnn_ref(x, edge_index, W1, b1, gamma, beta, W2, b2):
        import jax, jax.numpy as jnp
        import numpy as np
        N_NODES = 6250
        N_EDGES = 20000
        D_IN, D_HID, D_OUT = (256, 1024, 256)
        BN_EPS = 1e-05
        src, dst = (edge_index[0], edge_index[1])
        agg = jax.ops.segment_sum(x[src], dst, num_segments=x.shape[0])
        h = agg + x
        h1 = h @ W1 + b1
        mean = jnp.mean(h1, axis=0)
        var = jnp.mean(jnp.square(h1 - mean), axis=0)
        h1 = (h1 - mean) * jax.lax.rsqrt(var + BN_EPS) * gamma + beta
        h1 = jax.nn.relu(h1)
        out = jax.nn.relu(h1 @ W2 + b2)
        return out

    def _L1_gnn_ref(x, edge_index, W1, b1, W2, b2, W3, b3):
        import jax, jax.numpy as jnp
        import numpy as np
        N, E, D, H = (625, 20000, 256, 256)
        n = x.shape[0]
        loop = jnp.arange(n, dtype=edge_index.dtype)
        src = jnp.concatenate([edge_index[0], loop])
        dst = jnp.concatenate([edge_index[1], loop])
        deg = jax.ops.segment_sum(jnp.ones_like(dst, jnp.float32), dst, num_segments=n)
        dinv = jnp.where(deg > 0, jax.lax.rsqrt(deg), 0.0)
        norm = dinv[src] * dinv[dst]

        def layer(h, W, b):
            h = h @ W.T
            msg = h[src] * norm[:, None]
            agg = jax.ops.segment_sum(msg, dst, num_segments=n)
            return jax.nn.relu(agg + b)
        h = layer(x, W1, b1)
        h = layer(h, W2, b2)
        h = layer(h, W3, b3)
        return h
    edge_index = jnp.stack([src, dst])
    x = _layernorm(x + _L0_gnn_ref(x, edge_index, L0_gnn_W1, L0_gnn_b1, L0_gnn_gamma, L0_gnn_beta, L0_gnn_W2, L0_gnn_b2), axis=-1)
    x = _layernorm(x + _L1_gnn_ref(x, edge_index, L1_gnn_W1, L1_gnn_b1, L1_gnn_W2, L1_gnn_b2, L1_gnn_W3, L1_gnn_b3), axis=-1)
    return x

_drawn_inputs = setup_inputs


def setup_inputs(seed=0):
    import zlib

    import numpy as np

    out = dict(_drawn_inputs(seed))
    spreads = {'L0_gnn_b1': (0.0, 0.8),
     'L0_gnn_gamma': (1.0, 0.2),
     'L0_gnn_beta': (0.0, 0.1),
     'L0_gnn_b2': (0.0, 0.1),
     'L1_gnn_b1': (0.0, 0.314),
     'L1_gnn_b2': (0.0, 0.1),
     'L1_gnn_b3': (0.0, 0.1)}
    factors = {}
    for name, (base, spread) in spreads.items():
        noise = np.random.default_rng([zlib.crc32(name.encode()), seed]).standard_normal(out[name].shape)
        drawn = base * np.exp(spread * noise) if base else spread * noise
        out[name] = jnp.asarray(drawn.astype(out[name].dtype))
    for name, factor in factors.items():
        out[name] = (out[name] * factor).astype(out[name].dtype)
    return out
```

```python
from contextlib import ExitStack

import concourse.bass as bass
from concourse import mybir

F32 = mybir.dt.float32
I32 = mybir.dt.int32
U32 = mybir.dt.uint32
ALU = mybir.AluOpType
ACT = mybir.ActivationFunctionType
AX_X = mybir.AxisListType.X

P = 128
TILES = 8
SLOTS = 4
WIN = 128
CHUNK = 256
PAD_DST = 8192
EPS = 1e-5


def gnn_kernel(nc, x, src, dst, w1, b1, gamma, beta, w2, b2, wl, bl, out):
    N, D = x.shape
    E = src.shape[0]
    HID = w1.shape[1]
    DH, HT = D // P, HID // P
    GE = TILES * P
    NG = -(-E // GE)
    TAIL = E - (NG - 1) * GE
    NWIN = -(-N // WIN)
    NCOL = max(N, NWIN * WIN) + WIN
    NB = -(-N // P)
    NCH = N // CHUNK
    REM = N - NCH * CHUNK
    BPC = CHUNK // P
    assert NG % SLOTS == 0 and NG <= P and NCH % 2 == 0 and 0 < REM <= P and D == 2 * P and HT % 2 == 0
    assert N < PAD_DST - WIN

    x1_d = nc.dram_tensor("x1_d", (N, D), F32).ap()
    table_d = nc.dram_tensor("table_d", (N, D), F32).ap()

    with ExitStack() as ctx:
        def sb(name, shape, dt=F32):
            return ctx.enter_context(nc.sbuf_tensor(name, shape, dt))

        def sem(name):
            return ctx.enter_context(nc.semaphore(name))

        banks = [ctx.enter_context(nc.psum_tensor(f"bank{i}", [P, 512], F32)) for i in range(8)]

        iota = sb("iota", [P, P])
        iota1 = sb("iota1", [P, P])
        iotap = sb("iotap", [P, 1])
        ident = sb("ident", [P, P])
        before = sb("before", [NG, NG])
        ones = sb("ones", [P, 1])
        eps = sb("eps", [P, 1])
        w1_s = sb("w1_s", [P, DH, HID])
        w2_s = sb("w2_s", [P, HT, D])
        wraw = sb("wraw", [P, 3, DH, D])
        wt_s = sb("wt_s", [P, 3, DH, D])
        bnrow = sb("bnrow", [3 * HT, P])
        bncol = sb("bncol", [P, 3 * HT])
        bias_bc = sb("bias_bc", [P, 4, D])
        idx = sb("idx", [P, NG, TILES], I32)
        rel = sb("rel", [P, NG, TILES])
        dst1 = sb("dst1", [P, NG, TILES])
        ctl = sb("ctl", [1, NG, 4], I32)
        acc = sb("acc", [P, DH, NCOL])
        degrow = sb("degrow", [1, NCOL])
        ring = sb("ring", [P, SLOTS, TILES, D])
        idxbuf = sb("idxbuf", [P, SLOTS, TILES], I32)
        hot = sb("hot", [P, 2, TILES, WIN])
        hotx = sb("hotx", [P, TILES, WIN])
        relx = sb("relx", [P, 2, TILES])
        deg = sb("deg", [NB, P])
        degsum = sb("degsum", [P, NB])
        degroot = sb("degroot", [P, NB])
        dinv = sb("dinv", [P, NB])
        stats = sb("stats", [P, HT, NCH + 1, 6])
        bnmv = sb("bnmv", [P, HT, 2])
        bntmp = sb("bntmp", [P, 3, HT])
        bnscale = sb("bnscale", [P, HT])
        bnbias = sb("bnbias", [P, HT])
        xs = sb("xs", [P, 2, BPC, D])
        x1s = sb("x1s", [P, 2, BPC, D])
        ts = sb("ts", [P, 2, BPC, D])
        us = sb("us", [P, 2, DH, CHUNK])
        yt = sb("yt", [P, BPC, D])
        lnst = sb("lnst", [P, BPC, 6])
        lnmv = sb("lnmv", [P, BPC, 2])
        lnstd = sb("lnstd", [P, BPC])
        lnrec = sb("lnrec", [P, BPC])

        flat = ring[:, :, :, :].rearrange("p s t d -> p (s t d)")

        def stage(i):
            return flat[0:NG, i * GE:(i + 1) * GE]
        dst_i, src_i = stage(0).bitcast(I32), stage(1).bitcast(I32)
        dst_f, src_f, rel_f, dst1_f = stage(2), stage(3), stage(4), stage(5)
        mask_f = stage(6)
        gcol = sb("gcol", [NG, 6])
        hT = flat[:, 0:2 * HT * CHUNK].rearrange("p (b m n) -> p b m n", b=2, m=HT)

        s_const = sem("s_const")
        s_edge = sem("s_edge")
        s_wts = sem("s_wts")
        s_setup = sem("s_setup")
        s_edgef = sem("s_edgef")
        s_ptr = sem("s_ptr")
        s_idx = sem("s_idx")
        s_xl = [sem(f"s_xl{i}") for i in range(2)]
        s_xt = sem("s_xt")
        s_ainit = sem("s_ainit")
        s_wtp = sem("s_wtp")
        s_wtc = sem("s_wtc")
        s_bn = sem("s_bn")
        s_bnst = sem("s_bnst")
        s_degl = sem("s_degl")
        s_degt = sem("s_degt")
        s_deg = sem("s_deg")
        s_rt = sem("s_rt")

        s_apart = sem("s_apart")

        aggs = [{
            "idxbuf": sem(f"s_idxbuf{a}"),
            "rows": [sem(f"s_rows{a}_{q}") for q in range(SLOTS)],
            "hot": sem(f"s_hot{a}"),
            "sum": sem(f"s_sum{a}"),
            "acc": sem(f"s_acc{a}"),
            "hotx": sem(f"s_hotx{a}"), "sumx": sem(f"s_sumx{a}"), "accx": sem(f"s_accx{a}"),
        } for a in range(4)]
        dense = [{
            "chunk": sem(f"s_chunk{a}"),
            "h": sem(f"s_h{a}"),
            "relu": sem(f"s_relu{a}"),
            "y": sem(f"s_y{a}"),
            "v": sem(f"s_v{a}"),
            "std": sem(f"s_std{a}"),
            "xl": [sem(f"s_dxl{a}_{i}") for i in range(2)],
            "st": [sem(f"s_st{a}_{i}") for i in range(2)],
            "tt": sem(f"s_tt{a}"),
            "self": sem(f"s_self{a}"),
        } for a in range(4)]
        STEPS = [7, 2, 2, 6]
        ADDED, NORMED = 2, 4
        HP = HT // 2

        block = ctx.enter_context(nc.Block())

        def wait(eng, s, n):
            if not isinstance(n, int) or n > 0:
                eng.wait_ge(s, n)

        def wait_apart(eng, s, n):
            wait(eng, s, n)
            if not isinstance(n, int):
                eng.sem_inc(s_apart)

        def order(eng, s):
            n = [0]

            def step(ins):
                n[0] += 1
                ins.then_inc(s, 1)
                eng.wait_ge(s, n[0])
            return step

        def groups(eng, body, between=None):
            body(0, False)
            if between is not None:
                between()
            with eng.Fori(1, NG // SLOTS - 1) as i:
                body(i, False)
            body(NG // SLOTS - 1, True)

        def chunks(eng, body):
            for u in range(2):
                body(u, u, CHUNK, 0)
            with eng.Fori(1, NCH // 2) as i:
                for u in range(2):
                    body(i * 2 + u, u, CHUNK, i)
            body(NCH, 0, REM, NCH // 2)

        def cols(c, n):
            return bass.ds(c * CHUNK, n)

        def blocks(n):
            return [(b, min(P, n - b * P)) for b in range(-(-n // P))]

        def rows_of(t, c, n):
            v = t[bass.ds(c * CHUNK, n), :]
            return v.rearrange("(b p) d -> p b d", p=P) if n == CHUNK else v

        def tile_of(buf, u, n):
            return buf[:, u, :, :] if n == CHUNK else buf[0:n, u, 0, :]

        def halves(bank, n):
            return bank[:, :].rearrange("p (h n) -> p h n", h=DH)[:, :, 0:n]

        def stored(eng, a, per):
            eng.wait_ge(dense[a]["st"][0], 16 * per * (NCH // 2 + 1))
            eng.wait_ge(dense[a]["st"][1], 16 * per * (NCH // 2))

        @block.sync
        def _(sp):
            sp.wait_ge(s_const, 1)
            for t, e in ((dst_i, dst), (src_i, src)):
                sp.dma_start(t[0:NG - 1, :], e[0:(NG - 1) * GE].rearrange("(g e) -> g e", e=GE)).then_inc(s_edge, 16)
                sp.dma_start(t[NG - 1:NG, 0:TAIL], e[(NG - 1) * GE:E].rearrange("(a e) -> a e", a=1)).then_inc(s_edge, 16)

            def load_x(c, u, n, i):
                wait(sp, s_xt, c - 1)
                sp.dma_start(tile_of(xs, u, n), rows_of(x, c, n)).then_inc(s_xl[u], 16)
            chunks(sp, load_x)

            sp.dma_start(w1_s[:, :, :], w1.rearrange("(h p) n -> p h n", p=P)).then_inc(s_wts, 16)
            sp.dma_start(w2_s[:, :, :], w2.rearrange("(m p) n -> p m n", p=P)).then_inc(s_wts, 16)
            for l in range(3):
                sp.dma_start(wraw[:, l, :, :], wl[l].rearrange("(h p) n -> p h n", p=P)).then_inc(s_wts, 16)
            for i, v in enumerate((b1, gamma, beta)):
                sp.dma_start(bnrow[i * HT:(i + 1) * HT, :], v.rearrange("(m p) -> m p", p=P)).then_inc(s_wts, 16)
            for i, v in enumerate((b2, *bl)):
                sp.dma_start(bias_bc[:, i, :], v.rearrange("(a n) -> a n", a=1).to_broadcast([P, D])).then_inc(s_wts, 16)

            sp.wait_ge(aggs[0]["acc"], NG)
            sp.wait_ge(s_const, 2)
            full = (NB - 1) * P
            sp.dma_start(deg[0:NB - 1, :], degrow[0:1, 0:full]).then_inc(s_degl, 16)
            sp.dma_start(deg[NB - 1:NB, 0:N - full], degrow[0:1, full:N]).then_inc(s_degl, 16)

            def dense_io(a, source, stores):
                d, K = dense[a], STEPS[a]

                def load(c, u, n, i):
                    if source is not None:
                        wait(sp, d["v"], (c - 2) * K + ADDED)
                        sp.dma_start(tile_of(xs, u, n), rows_of(source, c, n)).then_inc(d["xl"][u], 16)

                def store(c, u, n):
                    sp.wait_ge(d["v"], c * K + K)
                    for buf, t in stores:
                        sp.dma_start(rows_of(t, c, n), tile_of(buf, u, n)).then_inc(d["st"][u], 16)

                def body(c, u, n, i):
                    load(c, u, n, i)
                    if not isinstance(c, int) or c > 0:
                        store(c - 1, 1 - u, CHUNK)
                chunks(sp, body)
                store(NCH, 0, REM)

            dense_io(0, x, ((x1s, x1_d), (ts, table_d)))
            dense_io(1, None, ((ts, table_d),))
            dense_io(2, None, ((ts, table_d),))
            dense_io(3, x1_d, ((x1s, out),))
            stored(sp, 3, 1)

        @block.gpsimd
        def _(pool):
            first = TAIL // P * P
            pool.memset(src_i[:, first:GE], 0)
            pool.memset(dst_i[:, first:GE], PAD_DST).then_inc(s_const, 1)
            pool.memset(degrow[:, :], 0.0)
            pool.memset(deg[:, :], 0.0)
            for t, base, step, cm in ((iota, 0, 1, 0), (iota1, 1, 1, 0), (iotap, 0, 0, 1)):
                pool.iota(t[:, :], pattern=[[step, t.shape[1]]], base=base, channel_multiplier=cm,
                          allow_small_or_imprecise_dtypes=True)
            pool.memset(ones[:, :], 1.0)
            pool.memset(eps[:, :], EPS)
            pool.memset(acc[:, :, N:NCOL], 0.0).then_inc(s_const, 1)

            def gather(a, table):
                g = aggs[a]

                def body(i, last):
                    for q in range(SLOTS):
                        k = i * SLOTS + q
                        wait(pool, g["sum"], k + 1 - SLOTS)
                        wait_apart(pool, g["idxbuf"], k + 1)
                        for j in range(TILES):
                            at = bass.IndirectOffsetOnAxis(ap=idxbuf[:, q, j:j + 1].bitcast(U32), axis=0)
                            pool.indirect_dma_start(out=ring[:, q, j, :], out_offset=None, in_=table[:, :],
                                                    in_offset=at).then_inc(g["rows"][q], 16)
                groups(pool, body)

            def take_chunks(a):
                d = dense[a]
                pool.wait_ge(aggs[a]["acc"], NG)

                def body(c, u, n, i):
                    wait(pool, d["y"], c - 1)
                    pool.tensor_copy(us[:, u, :, 0:n], acc[:, :, cols(c, n)]).then_inc(d["chunk"], 1)
                chunks(pool, body)

            gather(0, x)
            stored(pool, 0, 2)
            gather(1, table_d)
            take_chunks(1)
            stored(pool, 1, 1)
            gather(2, table_d)
            take_chunks(2)
            stored(pool, 2, 1)
            gather(3, table_d)
            take_chunks(3)

        @block.scalar
        def _(act):
            def init_acc(c, u, n, i):
                act.wait_ge(s_xt, c + 1)
                act.copy(acc[:, :, cols(c, n)], halves(banks[u], n)).then_inc(s_ainit, 1)

            def start():
                chunks(act, init_acc)
                for l in range(3):
                    act.wait_ge(s_wtp, l + 1)
                    act.copy(wt_s[:, l, :, :], halves(banks[2 + l], D)).then_inc(s_wtc, 1)
                act.wait_ge(s_wtp, 4)
                act.copy(bncol[:, :], banks[7][:, 0:3 * HT]).then_inc(s_wtc, 1)

            def indices(a, between=None):
                g = aggs[a]

                def body(i, last):
                    for q in range(SLOTS):
                        wait(act, g["rows"][q], i * (16 * TILES))
                        act.copy(idxbuf[:, q, :], idx[:, i * SLOTS + q, :]).then_inc(g["idxbuf"], 1)
                groups(act, body, between)

            def own_term(a, c, u, n):
                d = dense[a]
                act.wait_ge(d["tt"], c + 1)
                act.copy(acc[:, :, cols(c, n)], halves(banks[5 + u], n)).then_inc(d["self"], 1)

            def roots(a, c, n):
                d = dense[a]
                rows, nb = min(n, P), len(blocks(n))
                act.wait_ge(d["v"], c * STEPS[a] + NORMED)
                act.activation(lnstd[0:rows, 0:nb], lnmv[0:rows, 0:nb, 1], ACT.Sqrt,
                               bias=eps[0:rows, :]).then_inc(d["std"], 1)

            act.wait_ge(s_idx, 7)
            indices(0, start)
            act.wait_ge(s_deg, 1)
            act.activation(degroot[:, :], degsum[:, :], ACT.Sqrt).then_inc(s_rt, 1)
            act.wait_ge(s_deg, 3)
            act.activation(bntmp[:, 0, :], bnmv[:, :, 1], ACT.Sqrt, bias=eps[:, :]).then_inc(s_rt, 1)
            act.wait_ge(s_deg, 9)

            def mlp(c, u, n, i):
                d = dense[0]
                later = not isinstance(c, int) or c > 0
                for pr in range(HP):
                    act.wait_ge(d["h"], c * HP + pr + 1)
                    for e in range(2):
                        m = 2 * pr + e
                        ins = act.activation(hT[:, u, m, 0:n], banks[pr % 2][:, e * CHUNK:e * CHUNK + n], ACT.Relu,
                                             scale=bnscale[:, m:m + 1], bias=bnbias[:, m:m + 1])
                    ins.then_inc(d["relu"], 1)
                    if pr == 0 and later:
                        roots(0, c - 1, CHUNK)
                if later:
                    own_term(0, c - 1, 1 - u, CHUNK)
            chunks(act, mlp)
            roots(0, NCH, REM)
            own_term(0, NCH, 0, REM)
            for a in (1, 2):
                indices(a)
                chunks(act, lambda c, u, n, i: own_term(a, c, u, n))
            indices(3)
            chunks(act, lambda c, u, n, i: roots(3, c, n))

        @block.tensor
        def _(pe):
            pe.wait_ge(s_edgef, 1)
            for i, t in enumerate((src_f, rel_f, dst1_f)):
                for j in range(TILES):
                    ins = pe.transpose(banks[2 * i + j // 4][:, (j % 4) * P:(j % 4) * P + NG],
                                       t[:, j * P:(j + 1) * P], ident[0:NG, 0:NG])
                    if j % 4 == 3:
                        ins.then_inc(s_ptr, 1)
            pe.matmul(banks[6][0:1, 0:NG], gcol[:, 0:1], ident[0:NG, 0:NG], start=True, stop=True)
            pe.matmul(banks[6][0:1, P:P + NG], gcol[:, 3:4], ident[0:NG, 0:NG], start=True, stop=True)
            pe.matmul(banks[6][0:1, 2 * P:2 * P + NG], gcol[:, 3:4], before[:, :], start=True, stop=True).then_inc(s_ptr, 1)

            pe.wait_ge(s_idx, 7)

            def transpose_x(c, u, n, i):
                pe.wait_ge(s_xl[u], i * 16 + 16)
                wait(pe, s_ainit, c - 1)
                for b, rows in blocks(n):
                    for h in range(DH):
                        at = h * CHUNK + b * P
                        ins = pe.transpose(banks[u][:, at:at + rows], xs[0:rows, u, b, h * P:(h + 1) * P],
                                           ident[0:rows, 0:rows])
                ins.then_inc(s_xt, 1)
            chunks(pe, transpose_x)

            pe.wait_ge(s_wts, 16 * 12)
            for l in range(3):
                for ih in range(DH):
                    for oh in range(DH):
                        at = ih * D + oh * P
                        ins = pe.transpose(banks[2 + l][:, at:at + P], wraw[:, l, oh, ih * P:(ih + 1) * P], ident[:, :])
                ins.then_inc(s_wtp, 1)
            pe.transpose(banks[7][:, 0:3 * HT], bnrow[:, :], ident[0:3 * HT, 0:3 * HT]).then_inc(s_wtp, 1)
            pe.wait_ge(s_wtc, 4)

            def sums(a, bank, rows, hots, signal):
                if a == 0:
                    for j in range(TILES):
                        pe.matmul(bank[0:1, DH * WIN:DH * WIN + WIN], ones[:, :], hots[:, j, :],
                                  start=(j == 0), stop=(j == TILES - 1))
                for h in range(DH):
                    for j in range(TILES):
                        ins = pe.matmul(bank[:, h * WIN:(h + 1) * WIN], rows[:, j, h * P:(h + 1) * P], hots[:, j, :],
                                        start=(j == 0), stop=(j == TILES - 1))
                ins.then_inc(signal, 1)

            def aggregate(a):
                g = aggs[a]

                def body(i, last):
                    for q in range(SLOTS):
                        k = i * SLOTS + q
                        wide = pe.value_load(ctl[0:1, k, 1:2], min_val=0, max_val=1)
                        pe.wait_ge(g["hot"], k + 1)
                        pe.wait_ge(g["rows"][q], i * (16 * TILES) + 16 * TILES)
                        with pe.If(wide > 0):
                            done = pe.value_load(ctl[0:1, k, 2:3], min_val=0, max_val=NWIN * NG)
                            with pe.Fori(0, NWIN) as w:
                                pe.wait_ge(g["hotx"], done + w + 1)
                                sums(a, banks[7], ring[:, q, :, :], hotx, g["sumx"])
                        wait(pe, g["acc"], k - 1)
                        sums(a, banks[5 + q % 2], ring[:, q, :, :], hot[:, q % 2, :, :], g["sum"])
                groups(pe, body)

            def hidden(c, n, s, free, pairs_done):
                for pr in range(HP):
                    wait(pe, free, c * HP + pr - 1)
                    for e in range(2):
                        m = 2 * pr + e
                        for h in range(DH):
                            ins = pe.matmul(banks[pr % 2][:, e * CHUNK:e * CHUNK + n], w1_s[:, h, m * P:(m + 1) * P],
                                            acc[:, h, cols(c, n)], start=(h == 0), stop=(h == DH - 1))
                    ins.then_inc(s, 1)

            def transpose_rows(a, c, u, n):
                d = dense[a]
                pe.wait_ge(d["v"], c * STEPS[a] + STEPS[a])
                wait(pe, d["self"], c - 1)
                for b, rows in blocks(n):
                    for h in range(DH):
                        at = h * CHUNK + b * P
                        ins = pe.transpose(banks[5 + u][:, at:at + rows], ts[0:rows, u, b, h * P:(h + 1) * P],
                                           ident[0:rows, 0:rows])
                ins.then_inc(d["tt"], 1)

            def layer(a):
                d = dense[a]

                def body(c, u, n, i):
                    pe.wait_ge(d["chunk"], c + 1)
                    wait(pe, d["v"], (c - 2) * STEPS[a] + 1)
                    for b, rows in blocks(n):
                        for h in range(DH):
                            ins = pe.matmul(banks[2 + u][0:rows, b * D:(b + 1) * D], us[:, u, h, b * P:b * P + rows],
                                            wt_s[:, a - 1, h, :], start=(h == 0), stop=(h == DH - 1))
                    ins.then_inc(d["y"], 1)
                    if a < 3 and (not isinstance(c, int) or c > 0):
                        transpose_rows(a, c - 1, 1 - u, CHUNK)
                chunks(pe, body)
                if a < 3:
                    transpose_rows(a, NCH, 0, REM)

            aggregate(0)
            pe.wait_ge(aggs[0]["acc"], NG)
            pe.wait_ge(s_degl, 32)
            pe.transpose(banks[2][:, 0:NB], deg[:, :], ident[0:NB, 0:NB]).then_inc(s_degt, 1)
            chunks(pe, lambda c, u, n, i: hidden(c, n, s_bn, s_bnst, 0))
            pe.wait_ge(s_bnst, HP * (NCH + 1))

            def mlp(c, u, n, i):
                d = dense[0]
                hidden(c, n, d["h"], d["relu"], 0)
                if not isinstance(c, int) or c > 0:
                    transpose_rows(0, c - 1, 1 - u, CHUNK)
                wait(pe, d["v"], (c - 2) * STEPS[0] + 1)
                for b, rows in blocks(n):
                    for m in range(HT):
                        if b == 0 and m % 2 == 0:
                            pe.wait_ge(d["relu"], c * HP + m // 2 + 1)
                        ins = pe.matmul(banks[2 + u][0:rows, b * D:(b + 1) * D], hT[:, u, m, b * P:b * P + rows],
                                        w2_s[:, m, :], start=(m == 0), stop=(m == HT - 1))
                ins.then_inc(d["y"], 1)
            chunks(pe, mlp)
            transpose_rows(0, NCH, 0, REM)
            for a in range(1, 4):
                aggregate(a)
                layer(a)

        @block.vector
        def _(dve):
            step = order(dve, s_setup)
            dve.wait_ge(s_const, 2)
            dve.tensor_scalar(before[:, :], iota[0:NG, 0:NG], iotap[0:NG, :], float(NWIN), ALU.is_gt, ALU.mult)
            dve.tensor_scalar(ident[:, :], iota[:, :], iotap[:, :], None, ALU.is_equal)
            dve.wait_ge(s_edge, 64)
            dve.tensor_copy(src_f, src_i)
            step(dve.tensor_copy(dst_f, dst_i))
            dve.tensor_reduce(gcol[:, 0:1], dst_f, AX_X, ALU.min)
            step(dve.scalar_tensor_tensor(out=mask_f, in0=dst_f, scalar=float(PAD_DST), in1=dst_f, op0=ALU.is_lt,
                                          op1=ALU.mult))
            step(dve.tensor_reduce(gcol[:, 1:2], mask_f, AX_X, ALU.max))
            dve.tensor_scalar(rel_f, dst_f, gcol[:, 0:1], None, ALU.subtract)
            dve.tensor_scalar(dst1_f, dst_f, 1.0, None, ALU.add)
            step(dve.tensor_tensor(gcol[:, 2:3], gcol[:, 1:2], gcol[:, 0:1], ALU.subtract))
            dve.tensor_scalar(gcol[:, 3:4], gcol[:, 2:3], float(WIN), None, ALU.is_ge).then_inc(s_edgef, 1)
            for n, t in enumerate((idx, rel, dst1)):
                for e in range(2):
                    dve.wait_ge(s_ptr, 2 * n + e + 1)
                    dve.tensor_copy(t[:, :, 4 * e:4 * e + 4].rearrange("p g t -> p t g"),
                                    banks[2 * n + e][:, :].rearrange("p (t g) -> p t g", g=P)[:, :, 0:NG]).then_inc(s_idx, 1)
            dve.wait_ge(s_ptr, 7)
            dve.tensor_copy(ctl[:, :, 0:3].rearrange("p g c -> p c g"),
                            banks[6][0:1, 0:3 * P].rearrange("p (c g) -> p c g", g=P)[:, :, 0:NG]).then_inc(s_idx, 1)

            def one_hot(out, at, numbers):
                return dve.tensor_tensor(out, at.unsqueeze(2).to_broadcast([P, TILES, WIN]),
                                         numbers[:, :].unsqueeze(1).to_broadcast([P, TILES, WIN]), ALU.is_equal)

            def add(a, start, bank):
                if a == 0:
                    to = degrow[0:1, bass.ds(start, WIN)]
                    dve.tensor_tensor(to, to, bank[0:1, DH * WIN:DH * WIN + WIN], ALU.add)
                to = acc[:, :, bass.ds(start, WIN)]
                return dve.tensor_tensor(to, to, bank[:, 0:DH * WIN].rearrange("p (h n) -> p h n", h=DH), ALU.add)

            def aggregate(a):
                g = aggs[a]

                def hot_of(k, slot):
                    wait(dve, g["sum"], k - 1)
                    one_hot(hot[:, slot, :, :], rel[:, k, :], iota).then_inc(g["hot"], 1)

                def body(i, last):
                    for q in range(SLOTS):
                        k = i * SLOTS + q
                        start = dve.value_load(ctl[0:1, k, 0:1], min_val=0, max_val=N - 1)
                        wide = dve.value_load(ctl[0:1, k, 1:2], min_val=0, max_val=1)
                        if not last or q < SLOTS - 1:
                            hot_of(k + 1, (q + 1) % 2)
                        wait_apart(dve, g["acc"], k)
                        with dve.If(wide > 0):
                            done = dve.value_load(ctl[0:1, k, 2:3], min_val=0, max_val=NWIN * NG)
                            dve.scalar_tensor_tensor(out=relx[:, 0, :], in0=rel[:, k, :], scalar=float(WIN),
                                                     in1=dst1[:, k, :], op0=ALU.is_ge, op1=ALU.mult)
                            dve.drain()
                            dve.tensor_scalar(relx[:, 1, :], relx[:, 0, :], float(WIN), None, ALU.add)
                            dve.drain()
                            with dve.Fori(0, NWIN) as w:
                                dve.tensor_scalar(relx[:, 1, :], relx[:, 1, :], -float(WIN), None, ALU.add)
                                dve.drain()
                                one_hot(hotx[:, :, :], relx[:, 1, :], iota1).then_inc(g["hotx"], 1)
                                dve.wait_ge(g["sumx"], done + w + 1)
                                add(a, w * WIN, banks[7]).then_inc(g["accx"], 1)
                                dve.wait_ge(g["accx"], done + w + 1)
                        dve.wait_ge(g["sum"], k + 1)
                        add(a, start, banks[5 + q % 2]).then_inc(g["acc"], 1)
                hot_of(0, 0)
                groups(dve, body)

            def rows_done(a, c, u, n, i):
                d, K = dense[a], STEPS[a]
                rows, bs = min(n, P), blocks(n)
                nb = len(bs)
                r = slice(0, rows)
                bank = banks[2 + u][r, 0:nb * D].rearrange("p (b d) -> p b d", d=D)
                y = yt[r, 0:nb, :]
                at = [0]

                def step(*ins, apart=False):
                    at[0] += 1
                    ins[-1].then_inc(d["v"], 1)
                    (wait_apart if apart else wait)(dve, d["v"], c * K + at[0])

                def scale(b):
                    return dinv[r, bass.ds(c * BPC + b, 1)]

                dve.wait_ge(d["y"], c + 1)
                if a == 0:
                    step(dve.tensor_tensor(y, bank, bias_bc[r, 0:1, :].to_broadcast([rows, nb, D]), ALU.add))
                else:
                    step(*[dve.scalar_tensor_tensor(out=yt[r, b, :], in0=bank[:, b, :], scalar=scale(b),
                                                    in1=bias_bc[r, a, :], op0=ALU.mult, op1=ALU.add) for b in range(nb)])
                if a in (1, 2):
                    wait(dve, d["st"][u], i * 16)
                    wait(dve, d["tt"], c - 1)
                    step(*[dve.tensor_scalar(ts[r, u, b, :], yt[r, b, :], 0.0, scale(b), ALU.max, ALU.mult)
                           for b in range(nb)])
                    return
                dve.wait_ge(d["xl"][u], i * 16 + 16)
                step(dve.scalar_tensor_tensor(out=y, in0=y, scalar=0.0, in1=xs[r, u, 0:nb, :], op0=ALU.max, op1=ALU.add))
                step(*[dve.bn_stats(lnst[r, b, :], yt[r, b, :]) for b in range(nb)], apart=True)
                step(*[dve.bn_aggr(lnmv[r, b, :], lnst[r, b, :]) for b in range(nb)])
                dve.wait_ge(d["std"], c + 1)
                step(dve.reciprocal(lnrec[r, 0:nb], lnstd[r, 0:nb]))
                wait(dve, d["st"][u], i * (32 if a == 0 else 16))
                step(*[dve.tensor_scalar(x1s[r, u, b, :], yt[r, b, :], lnmv[r, b, 0:1], lnrec[r, b:b + 1],
                                         ALU.subtract, ALU.mult) for b in range(nb)])
                if a == 0:
                    wait(dve, d["tt"], c - 1)
                    step(*[dve.tensor_scalar(ts[r, u, b, :], x1s[r, u, b, :], scale(b), None, ALU.mult)
                           for b in range(nb)])

            dve.wait_ge(s_ainit, NCH + 1)
            dve.wait_ge(s_setup, 4)
            aggregate(0)

            step = order(dve, s_deg)
            dve.wait_ge(s_degt, 1)
            step(dve.tensor_scalar(degsum[:, :], banks[2][:, 0:NB], 1.0, None, ALU.add))
            dve.wait_ge(s_rt, 1)
            step(dve.reciprocal(dinv[:, :], degroot[:, :]))

            def statistics(c, u, n, i):
                for pr in range(HP):
                    dve.wait_ge(s_bn, c * HP + pr + 1)
                    for e in range(2):
                        ins = dve.bn_stats(stats[:, 2 * pr + e, c, :], banks[pr % 2][:, e * CHUNK:e * CHUNK + n])
                    ins.then_inc(s_bnst, 1)
            chunks(dve, statistics)
            dve.wait_ge(s_bnst, HP * (NCH + 1))
            for m in range(HT):
                ins = dve.bn_aggr(bnmv[:, m, :], stats[:, m, :, :].rearrange("p c s -> p (c s)"))
            step(ins)
            dve.wait_ge(s_wtc, 4)
            dve.wait_ge(s_rt, 2)
            b1_c, gamma_c, beta_c = (bncol[:, i * HT:(i + 1) * HT] for i in range(3))
            step(dve.reciprocal(bntmp[:, 1, :], bntmp[:, 0, :]))
            step(dve.tensor_tensor(bnscale[:, :], bntmp[:, 1, :], gamma_c, ALU.mult))
            step(dve.tensor_tensor(bntmp[:, 0, :], bnmv[:, :, 0], b1_c, ALU.add))
            step(dve.tensor_tensor(bntmp[:, 2, :], b1_c, bntmp[:, 0, :], ALU.subtract))
            step(dve.tensor_tensor(bntmp[:, 1, :], bntmp[:, 2, :], bnscale[:, :], ALU.mult))
            step(dve.tensor_tensor(bnbias[:, :], bntmp[:, 1, :], beta_c, ALU.add))

            for a in range(4):
                if a > 0:
                    dve.wait_ge(dense[a - 1]["self"], NCH + 1)
                    aggregate(a)
                chunks(dve, lambda c, u, n, i: rows_done(a, c, u, n, i))


_INS = ['x', 'src', 'dst', 'L0_gnn_W1', 'L0_gnn_b1', 'L0_gnn_gamma', 'L0_gnn_beta', 'L0_gnn_W2', 'L0_gnn_b2',
        'L1_gnn_W1', 'L1_gnn_b1', 'L1_gnn_W2', 'L1_gnn_b2', 'L1_gnn_W3', 'L1_gnn_b3']


def kernel(**inputs):
    import numpy as _np
    import concourse.bacc as _bacc
    from concourse import mybir as _mybir
    from concourse.bass_utils import run_bass_kernel_spmd as _run

    nc = _bacc.Bacc("TRN2", target_bir_lowering=False, num_devices=1)
    arrays, t = {}, {}
    for name in _INS:
        a = _np.ascontiguousarray(inputs[name])
        arrays[f"in_{name}_dram"] = a
        t[name] = nc.dram_tensor(f"in_{name}_dram", a.shape, _mybir.dt.from_np(a.dtype), kind="ExternalInput").ap()
    out = nc.dram_tensor("out_0_dram", t["x"].shape, _mybir.dt.float32, kind="ExternalOutput").ap()
    gnn_kernel(nc, t["x"], t["src"], t["dst"], t["L0_gnn_W1"], t["L0_gnn_b1"], t["L0_gnn_gamma"], t["L0_gnn_beta"],
               t["L0_gnn_W2"], t["L0_gnn_b2"], [t[f"L1_gnn_W{i}"] for i in (1, 2, 3)],
               [t[f"L1_gnn_b{i}"] for i in (1, 2, 3)], out)
    r = _run(nc, [arrays], core_ids=[0])
    return r.results[0]["out_0_dram"]
```

```python
from contextlib import ExitStack

import concourse.bass as bass
from concourse import mybir

F32 = mybir.dt.float32
I32 = mybir.dt.int32
U32 = mybir.dt.uint32
ALU = mybir.AluOpType
ACT = mybir.ActivationFunctionType
AX_X = mybir.AxisListType.X

P = 128
TILES = 8
SLOTS = 4
LAG = 2
WIN = 128
CHUNK = 256
PAD_DST = 8192
EPS = 1e-5


def gnn_kernel(nc, x, src, dst, w1, b1, gamma, beta, w2, b2, wl, bl, out):
    N, D = x.shape
    E = src.shape[0]
    HID = w1.shape[1]
    DH, HT = D // P, HID // P
    GE = TILES * P
    NG = -(-E // GE)
    TAIL = E - (NG - 1) * GE
    NWIN = -(-N // WIN)
    NCOL = max(N, NWIN * WIN) + WIN
    NB = -(-N // P)
    NCH = N // CHUNK
    REM = N - NCH * CHUNK
    BPC = CHUNK // P
    NP = NG // (2 * SLOTS)
    REST = 2 * (NP - LAG)
    assert NG % (2 * SLOTS) == 0 and NG <= P and NCH % 2 == 0 and 0 < REM <= P and D == 2 * P and HT % 2 == 0
    assert NCH - REST == 2
    assert N < PAD_DST - WIN

    x1_d = nc.dram_tensor("x1_d", (N, D), F32).ap()
    tables = [nc.dram_tensor(f"table{i}_d", (N, D), F32).ap() for i in range(2)]
    h_d = nc.dram_tensor("h_d", ((NCH + 1) * P, HT * CHUNK), F32).ap()

    with ExitStack() as ctx:
        def sb(name, shape, dt=F32):
            return ctx.enter_context(nc.sbuf_tensor(name, shape, dt))

        def sem(name):
            return ctx.enter_context(nc.semaphore(name))

        banks = [ctx.enter_context(nc.psum_tensor(f"bank{i}", [P, 512], F32)) for i in range(8)]

        iota = sb("iota", [P, P])
        iota1 = sb("iota1", [P, P])
        iotap = sb("iotap", [P, 1])
        ident = sb("ident", [P, P])
        before = sb("before", [NG, NG])
        ones = sb("ones", [P, 1])
        eps = sb("eps", [P, 1])
        w1_s = sb("w1_s", [P, DH, HID])
        w2_s = sb("w2_s", [P, HT, D])
        wraw = sb("wraw", [P, 3, DH, D])
        wt_s = sb("wt_s", [P, 3, DH, D])
        bnrow = sb("bnrow", [3 * HT, P])
        bncol = sb("bncol", [P, 3 * HT])
        bias_bc = sb("bias_bc", [P, 4, D])
        idx = sb("idx", [P, NG, TILES], I32)
        rel = sb("rel", [P, NG + 1, TILES])
        dst1 = sb("dst1", [P, NG, TILES])
        ctl = sb("ctl", [1, NG, 4], I32)
        early = sb("early", [1, 1], I32)
        least = sb("least", [1, NG])
        late = sb("late", [1, 3, NG])
        acc = sb("acc", [P, DH, NCOL])
        degrow = sb("degrow", [1, NCOL])
        ring = sb("ring", [P, SLOTS, TILES, D])
        idxbuf = sb("idxbuf", [P, SLOTS, TILES], I32)
        hot = sb("hot", [P, 2, TILES, WIN])
        hotx = sb("hotx", [P, TILES, WIN])
        relx = sb("relx", [P, 2, TILES])
        deg = sb("deg", [NB, P])
        degsum = sb("degsum", [P, NB])
        degroot = sb("degroot", [P, NB])
        dinv = sb("dinv", [P, NB])
        stats = sb("stats", [P, HT, NCH + 1, 6])
        bnmv = sb("bnmv", [P, HT, 2])
        bntmp = sb("bntmp", [P, 3, HT])
        bnscale = sb("bnscale", [P, HT])
        bnbias = sb("bnbias", [P, HT])
        xs = sb("xs", [P, 2, BPC, D])
        x1s = sb("x1s", [P, 2, BPC, D])
        ts = sb("ts", [P, 2, BPC, D])
        hs = sb("hs", [P, 2, HT, CHUNK])
        us = sb("us", [P, 2, DH, CHUNK])
        yt = sb("yt", [P, BPC, D])
        lnst = sb("lnst", [P, BPC, 6])
        lnmv = sb("lnmv", [P, BPC, 2])
        lnstd = sb("lnstd", [P, BPC])
        lnrec = sb("lnrec", [P, BPC])

        flat = ring[:, :, :, :].rearrange("p s t d -> p (s t d)")

        def stage(i):
            return flat[0:NG, i * GE:(i + 1) * GE]
        dst_i, src_i = stage(0).bitcast(I32), stage(1).bitcast(I32)
        dst_f, src_f, rel_f, dst1_f = stage(2), stage(3), stage(4), stage(5)
        mask_f = stage(6)
        gcol = sb("gcol", [NG, 6])
        hT = flat[:, 0:2 * HT * CHUNK].rearrange("p (b m n) -> p b m n", b=2, m=HT)

        s_const = sem("s_const")
        s_edge = sem("s_edge")
        s_wts = sem("s_wts")
        s_setup = sem("s_setup")
        s_edgef = sem("s_edgef")
        s_ptr = sem("s_ptr")
        s_idx = sem("s_idx")
        s_wtp = sem("s_wtp")
        s_wtc = sem("s_wtc")
        s_xl = [sem(f"s_xl{i}") for i in range(2)]
        s_xt = sem("s_xt")
        s_own = sem("s_own")
        s_h = sem("s_h")
        s_stats = sem("s_stats")
        s_hs = sem("s_hs")
        s_hst = [sem(f"s_hst{i}") for i in range(2)]
        s_hl = [sem(f"s_hl{i}") for i in range(2)]
        s_degl = sem("s_degl")
        s_degt = sem("s_degt")
        s_deg = sem("s_deg")
        s_rt = sem("s_rt")

        s_apart = sem("s_apart")

        aggs = [{
            "idxbuf": sem(f"s_idxbuf{a}"),
            "rows": [sem(f"s_rows{a}_{q}") for q in range(SLOTS)],
            "hot": sem(f"s_hot{a}"),
            "sum": sem(f"s_sum{a}"),
            "acc": sem(f"s_acc{a}"),
            "hotx": sem(f"s_hotx{a}"), "sumx": sem(f"s_sumx{a}"), "accx": sem(f"s_accx{a}"),
        } for a in range(4)]
        dense = [{
            "chunk": sem(f"s_chunk{a}"),
            "relu": sem(f"s_relu{a}"),
            "y": sem(f"s_y{a}"),
            "v": sem(f"s_v{a}"),
            "std": sem(f"s_std{a}"),
            "xl": [sem(f"s_dxl{a}_{i}") for i in range(2)],
            "st": [sem(f"s_st{a}_{i}") for i in range(2)],
            "tt": sem(f"s_tt{a}"),
            "self": sem(f"s_self{a}"),
        } for a in range(4)]
        STEPS = [7, 2, 2, 6]
        ADDED, NORMED = 2, 4
        HP = HT // 2
        SUM0, ACC0 = SLOTS, 2

        block = ctx.enter_context(nc.Block())

        def wait(eng, s, n):
            if not isinstance(n, int) or n > 0:
                eng.wait_ge(s, n)

        def wait_apart(eng, s, n):
            wait(eng, s, n)
            if not isinstance(n, int):
                eng.sem_inc(s_apart)

        def order(eng, s):
            n = [0]

            def step(ins):
                n[0] += 1
                ins.then_inc(s, 1)
                eng.wait_ge(s, n[0])
            return step

        def if_early(eng, want):
            flag = eng.value_load(early[0:1, 0:1], min_val=0, max_val=1)
            return eng.If(flag > 0) if want else eng.If(flag < 1)

        def passes(eng, group, retire, rest, ahead=False):
            both = 2 * SLOTS
            behind = SLOTS if ahead else 0

            def some(i, gs):
                for g in gs:
                    group(i * both + g, g % SLOTS, i * 2 + g // SLOTS)
            if ahead:
                some(0, range(both))
            with eng.Fori(1 if ahead else 0, LAG + 1) as i:
                some(i, range(both))
            with if_early(eng, True):
                for u in range(2):
                    retire(u, u, 0, both * (LAG + 1) - behind)
            with eng.Fori(LAG + 1, NP) as i:
                for u in range(2):
                    some(i, range(u * SLOTS, (u + 1) * SLOTS))
                    with if_early(eng, True):
                        retire(i * 2 + (u - 2 * LAG), u, i - LAG, i * both + ((u + 1) * SLOTS - behind))
            with if_early(eng, False):
                for u in range(2):
                    retire(u, u, 0, NG)
                with eng.Fori(1, REST // 2) as i:
                    for u in range(2):
                        retire(i * 2 + u, u, i, NG)
            rest()

        LAST = [(NCH - 2, 0, CHUNK, NCH // 2 - 1), (NCH - 1, 1, CHUNK, NCH // 2 - 1), (NCH, 0, REM, NCH // 2)]

        def chunks(eng, body):
            for u in range(2):
                body(u, u, CHUNK, 0)
            with eng.Fori(1, NCH // 2) as i:
                for u in range(2):
                    body(i * 2 + u, u, CHUNK, i)
            body(NCH, 0, REM, NCH // 2)

        def cols(c, n):
            return bass.ds(c * CHUNK, n)

        def blocks(n):
            return [(b, min(P, n - b * P)) for b in range(-(-n // P))]

        def rows_of(t, c, n):
            v = t[bass.ds(c * CHUNK, n), :]
            return v.rearrange("(b p) d -> p b d", p=P) if n == CHUNK else v

        def tile_of(buf, u, n):
            return buf[:, u, :, :] if n == CHUNK else buf[0:n, u, 0, :]

        def halves(bank, n):
            return bank[:, :].rearrange("p (h n) -> p h n", h=DH)[:, :, 0:n]

        def hidden_at(c):
            return h_d[bass.ds(c * P, P), :]

        def stored(eng, a, per):
            eng.wait_ge(dense[a]["st"][0], 16 * per * (NCH // 2 + 1))
            eng.wait_ge(dense[a]["st"][1], 16 * per * (NCH // 2))

        @block.sync
        def _(sp):
            sp.wait_ge(s_const, 1)
            for t, e in ((dst_i, dst), (src_i, src)):
                sp.dma_start(t[0:NG - 1, :], e[0:(NG - 1) * GE].rearrange("(g e) -> g e", e=GE)).then_inc(s_edge, 16)
                sp.dma_start(t[NG - 1:NG, 0:TAIL], e[(NG - 1) * GE:E].rearrange("(a e) -> a e", a=1)).then_inc(s_edge, 16)

            sp.dma_start(w1_s[:, :, :], w1.rearrange("(h p) n -> p h n", p=P)).then_inc(s_wts, 16)
            sp.dma_start(w2_s[:, :, :], w2.rearrange("(m p) n -> p m n", p=P)).then_inc(s_wts, 16)
            for l in range(3):
                sp.dma_start(wraw[:, l, :, :], wl[l].rearrange("(h p) n -> p h n", p=P)).then_inc(s_wts, 16)
            for i, v in enumerate((b1, gamma, beta)):
                sp.dma_start(bnrow[i * HT:(i + 1) * HT, :], v.rearrange("(m p) -> m p", p=P)).then_inc(s_wts, 16)
            for i, v in enumerate((b2, *bl)):
                sp.dma_start(bias_bc[:, i, :], v.rearrange("(a n) -> a n", a=1).to_broadcast([P, D])).then_inc(s_wts, 16)

            def store_hidden(c, u):
                sp.wait_ge(s_hs, c * HP + HP)
                sp.dma_start(hidden_at(c), hs[:, u, :, :].rearrange("p m n -> p (m n)")).then_inc(s_hst[u], 16)

            def hidden_io(c, u, n, i):
                wait(sp, s_xt, c - 1)
                sp.dma_start(tile_of(xs, u, n), rows_of(x, c, n)).then_inc(s_xl[u], 16)
                if not isinstance(c, int) or c > 0:
                    store_hidden(c - 1, 1 - u)
            chunks(sp, hidden_io)
            store_hidden(NCH, 0)

            sp.wait_ge(aggs[0]["acc"], ACC0 + NG)
            sp.wait_ge(s_const, 2)
            full = (NB - 1) * P
            sp.dma_start(deg[0:NB - 1, :], degrow[0:1, 0:full]).then_inc(s_degl, 16)
            sp.dma_start(deg[NB - 1:NB, 0:N - full], degrow[0:1, full:N]).then_inc(s_degl, 16)

            def dense_io(a, source, stores):
                d, K = dense[a], STEPS[a]

                def load(c, u, n, i):
                    if source is not None:
                        wait(sp, d["v"], (c - 2) * K + ADDED)
                        sp.dma_start(tile_of(xs, u, n), rows_of(source, c, n)).then_inc(d["xl"][u], 16)

                def store(c, u, n):
                    sp.wait_ge(d["v"], c * K + K)
                    for buf, t in stores:
                        sp.dma_start(rows_of(t, c, n), tile_of(buf, u, n)).then_inc(d["st"][u], 16)

                def body(c, u, n, i):
                    load(c, u, n, i)
                    if not isinstance(c, int) or c > 0:
                        store(c - 1, 1 - u, CHUNK)
                chunks(sp, body)
                store(NCH, 0, REM)

            dense_io(0, x, ((x1s, x1_d), (ts, tables[0])))
            dense_io(1, None, ((ts, tables[1]),))
            dense_io(2, None, ((ts, tables[0]),))
            dense_io(3, x1_d, ((x1s, out),))
            stored(sp, 3, 1)

        @block.gpsimd
        def _(pool):
            first = TAIL // P * P
            pool.memset(src_i[:, first:GE], 0)
            pool.memset(dst_i[:, first:GE], PAD_DST).then_inc(s_const, 1)
            pool.memset(degrow[:, :], 0.0)
            pool.memset(deg[:, :], 0.0)
            for t, base, step, cm in ((iota, 0, 1, 0), (iota1, 1, 1, 0), (iotap, 0, 0, 1)):
                pool.iota(t[:, :], pattern=[[step, t.shape[1]]], base=base, channel_multiplier=cm,
                          allow_small_or_imprecise_dtypes=True)
            pool.iota(least[:, :], pattern=[[CHUNK, NG // SLOTS], [0, SLOTS]], base=(1 - 2 * LAG) * CHUNK,
                      channel_multiplier=0, allow_small_or_imprecise_dtypes=True)
            pool.memset(rel[:, NG, :], float(PAD_DST))
            pool.memset(ones[:, :], 1.0)
            pool.memset(eps[:, :], EPS).then_inc(s_const, 1)

            def gather(a, table):
                g = aggs[a]

                with pool.Fori(0, NG // SLOTS) as i:
                    for q in range(SLOTS):
                        k = i * SLOTS + q
                        pool.wait_ge(g["sum"], SUM0 + k + 1 - SLOTS)
                        wait_apart(pool, g["idxbuf"], k + 1)
                        for j in range(TILES):
                            at = bass.IndirectOffsetOnAxis(ap=idxbuf[:, q, j:j + 1].bitcast(U32), axis=0)
                            pool.indirect_dma_start(out=ring[:, q, j, :], out_offset=None, in_=table[:, :],
                                                    in_offset=at).then_inc(g["rows"][q], 16)

            gather(0, x)
            pool.wait_ge(s_hst[0], 16 * (NCH // 2 + 1))
            pool.wait_ge(s_hst[1], 16 * (NCH // 2))

            def load_hidden(c, u, n, i):
                wait(pool, dense[0]["relu"], c - 1)
                pool.dma_start(hs[:, u, :, :].rearrange("p m n -> p (m n)"), hidden_at(c)).then_inc(s_hl[u], 16)
            chunks(pool, load_hidden)
            stored(pool, 0, 2)
            gather(1, tables[0])
            stored(pool, 1, 1)
            gather(2, tables[1])
            stored(pool, 2, 1)
            gather(3, tables[0])

        @block.scalar
        def _(act):
            def own_term(a, c, u, n):
                d = dense[a]
                wait_apart(act, d["tt"], c + 1)
                act.copy(acc[:, :, cols(c, n)], halves(banks[u], n)).then_inc(d["self"], 1)

            def roots(a, c, n):
                d = dense[a]
                rows, nb = min(n, P), len(blocks(n))
                act.wait_ge(d["v"], c * STEPS[a] + NORMED)
                act.activation(lnstd[0:rows, 0:nb], lnmv[0:rows, 0:nb, 1], ACT.Sqrt,
                               bias=eps[0:rows, :]).then_inc(d["std"], 1)

            def keep_hidden(c, u, n, i):
                wait(act, s_hst[u], i * 16)
                for pr in range(HP):
                    act.wait_ge(s_stats, c * HP + pr + 1)
                    act.copy(hs[:, u, 2 * pr:2 * pr + 2, 0:n],
                             banks[pr % 2][:, :].rearrange("p (e n) -> p e n", e=2)[:, :, 0:n]).then_inc(s_hs, 1)

            def take(a, c, u, n, need):
                d = dense[a]
                wait(act, d["y"], c - 1)
                wait_apart(act, aggs[a]["acc"], ACC0 + need)
                act.copy(us[:, u, :, 0:n], acc[:, :, cols(c, n)]).then_inc(d["chunk"], 1)

            def finish(a, c, u, n, i):
                if a == 0:
                    keep_hidden(c, u, n, i)
                elif a < 3:
                    own_term(a, c, u, n)
                else:
                    roots(a, c, n)

            def aggregate(a):
                g = aggs[a]

                def group(k, q, i):
                    wait(act, g["rows"][q], i * (16 * TILES))
                    act.copy(idxbuf[:, q, :], idx[:, k, :]).then_inc(g["idxbuf"], 1)

                def retire(c, u, i, need):
                    if a > 0:
                        take(a, c, u, CHUNK, need)
                    if not isinstance(c, int) or c > 0:
                        finish(a, c - 1, 1 - u, CHUNK, i if u else i - 1)

                def rest():
                    if a > 0:
                        take(a, *LAST[0][0:3], NG)
                    finish(a, REST - 1, 1, CHUNK, REST // 2 - 1)
                    if a > 0:
                        take(a, *LAST[1][0:3], NG)
                    finish(a, *LAST[0])
                    if a > 0:
                        take(a, *LAST[2][0:3], NG)
                    finish(a, *LAST[1])
                    finish(a, *LAST[2])
                passes(act, group, retire, rest, ahead=True)

            act.wait_ge(s_idx, 8)
            for l in range(3):
                act.wait_ge(s_wtp, l + 1)
                act.copy(wt_s[:, l, :, :], halves(banks[2 + l], D)).then_inc(s_wtc, 1)
            act.wait_ge(s_wtp, 4)
            act.copy(bncol[:, :], banks[7][:, 0:3 * HT]).then_inc(s_wtc, 1)
            aggregate(0)
            act.wait_ge(s_deg, 1)
            act.activation(degroot[:, :], degsum[:, :], ACT.Sqrt).then_inc(s_rt, 1)
            act.wait_ge(s_deg, 3)
            act.activation(bntmp[:, 0, :], bnmv[:, :, 1], ACT.Sqrt, bias=eps[:, :]).then_inc(s_rt, 1)
            act.wait_ge(s_deg, 9)

            def mlp(c, u, n, i):
                d = dense[0]
                act.wait_ge(s_hl[u], i * 16 + 16)
                wait(act, d["y"], c - 1)
                for m in range(HT):
                    ins = act.activation(hT[:, u, m, 0:n], hs[:, u, m, 0:n], ACT.Relu,
                                         scale=bnscale[:, m:m + 1], bias=bnbias[:, m:m + 1])
                ins.then_inc(d["relu"], 1)
                if not isinstance(c, int) or c > 1:
                    own_term(0, c - 2, u, CHUNK)
                if not isinstance(c, int) or c > 0:
                    roots(0, c - 1, CHUNK)
            chunks(act, mlp)
            own_term(0, NCH - 1, 1, CHUNK)
            roots(0, NCH, REM)
            own_term(0, NCH, 0, REM)
            for a in range(1, 4):
                aggregate(a)

        @block.tensor
        def _(pe):
            pe.wait_ge(s_edgef, 1)
            for i, t in enumerate((src_f, rel_f, dst1_f)):
                for j in range(TILES):
                    ins = pe.transpose(banks[2 * i + j // 4][:, (j % 4) * P:(j % 4) * P + NG],
                                       t[:, j * P:(j + 1) * P], ident[0:NG, 0:NG])
                    if j % 4 == 3:
                        ins.then_inc(s_ptr, 1)
            pe.matmul(banks[6][0:1, 0:NG], gcol[:, 0:1], ident[0:NG, 0:NG], start=True, stop=True)
            pe.matmul(banks[6][0:1, P:P + NG], gcol[:, 3:4], ident[0:NG, 0:NG], start=True, stop=True)
            pe.matmul(banks[6][0:1, 2 * P:2 * P + NG], gcol[:, 3:4], before[:, :], start=True, stop=True).then_inc(s_ptr, 1)

            pe.wait_ge(s_idx, 8)

            pe.wait_ge(s_wts, 16 * 12)
            for l in range(3):
                for ih in range(DH):
                    for oh in range(DH):
                        at = ih * D + oh * P
                        ins = pe.transpose(banks[2 + l][:, at:at + P], wraw[:, l, oh, ih * P:(ih + 1) * P], ident[:, :])
                ins.then_inc(s_wtp, 1)
            pe.transpose(banks[7][:, 0:3 * HT], bnrow[:, :], ident[0:3 * HT, 0:3 * HT]).then_inc(s_wtp, 1)
            pe.wait_ge(s_wtc, 4)

            def sums(a, bank, rows, hots, signal):
                if a == 0:
                    for j in range(TILES):
                        pe.matmul(bank[0:1, DH * WIN:DH * WIN + WIN], ones[:, :], hots[:, j, :],
                                  start=(j == 0), stop=(j == TILES - 1))
                for h in range(DH):
                    for j in range(TILES):
                        ins = pe.matmul(bank[:, h * WIN:(h + 1) * WIN], rows[:, j, h * P:(h + 1) * P], hots[:, j, :],
                                        start=(j == 0), stop=(j == TILES - 1))
                ins.then_inc(signal, 1)

            def transpose(buf, bank, u, n):
                for b, rows in blocks(n):
                    for h in range(DH):
                        at = h * CHUNK + b * P
                        ins = pe.transpose(bank[:, at:at + rows], buf[0:rows, u, b, h * P:(h + 1) * P],
                                           ident[0:rows, 0:rows])
                return ins

            def hidden(c, u, n, i):
                pe.wait_ge(s_xl[u], i * 16 + 16)
                transpose(xs, banks[2 + u], u, n).then_inc(s_xt, 1)
                pe.wait_ge(s_own, c + 1)
                for pr in range(HP):
                    wait(pe, s_hs, c * HP + pr - 1)
                    for e in range(2):
                        m = 2 * pr + e
                        for h in range(DH):
                            ins = pe.matmul(banks[pr % 2][:, e * CHUNK:e * CHUNK + n], w1_s[:, h, m * P:(m + 1) * P],
                                            acc[:, h, cols(c, n)], start=(h == 0), stop=(h == DH - 1))
                    ins.then_inc(s_h, 1)

            def transpose_rows(a, c, u, n):
                d = dense[a]
                pe.wait_ge(d["v"], c * STEPS[a] + STEPS[a])
                wait(pe, d["self"], c - 1 if a > 0 else c)
                transpose(ts, banks[u], u, n).then_inc(d["tt"], 1)

            def layer(a, c, u, n):
                d = dense[a]
                pe.wait_ge(d["chunk"], c + 1)
                wait(pe, d["v"], (c - 2) * STEPS[a] + 1)
                for b, rows in blocks(n):
                    for h in range(DH):
                        ins = pe.matmul(banks[2 + u][0:rows, b * D:(b + 1) * D], us[:, u, h, b * P:b * P + rows],
                                        wt_s[:, a - 1, h, :], start=(h == 0), stop=(h == DH - 1))
                ins.then_inc(d["y"], 1)

            def aggregate(a):
                g = aggs[a]
                pe.sem_inc(g["sum"], SUM0)

                def group(k, q, i):
                    wide = pe.value_load(ctl[0:1, k, 1:2], min_val=0, max_val=1)
                    pe.wait_ge(g["hot"], k + 1)
                    pe.wait_ge(g["rows"][q], i * (16 * TILES) + 16 * TILES)
                    with pe.If(wide > 0):
                        done = pe.value_load(ctl[0:1, k, 2:3], min_val=0, max_val=NWIN * NG)
                        with pe.Fori(0, NWIN) as w:
                            pe.wait_ge(g["hotx"], done + w + 1)
                            sums(a, banks[7], ring[:, q, :, :], hotx, g["sumx"])
                    pe.wait_ge(g["acc"], ACC0 + k - 1)
                    sums(a, banks[5 + q % 2], ring[:, q, :, :], hot[:, q % 2, :, :], g["sum"])

                def retire(c, u, i, done):
                    if a == 0:
                        hidden(c, u, CHUNK, i)
                    else:
                        layer(a, c, u, CHUNK)
                        if a < 3:
                            transpose_rows(a, c, u, CHUNK)

                def rest():
                    if a == 0:
                        for chunk in LAST:
                            hidden(*chunk)
                        return
                    layer(a, *LAST[0][0:3])
                    layer(a, *LAST[1][0:3])
                    if a < 3:
                        transpose_rows(a, *LAST[0][0:3])
                    layer(a, *LAST[2][0:3])
                    if a < 3:
                        transpose_rows(a, *LAST[1][0:3])
                        transpose_rows(a, *LAST[2][0:3])
                passes(pe, group, retire, rest)

            aggregate(0)
            pe.wait_ge(s_degl, 32)
            pe.transpose(banks[4][:, 0:NB], deg[:, :], ident[0:NB, 0:NB]).then_inc(s_degt, 1)

            def mlp(c, u, n, i):
                d = dense[0]
                pe.wait_ge(d["relu"], c + 1)
                wait(pe, d["v"], (c - 2) * STEPS[0] + 1)
                for b, rows in blocks(n):
                    for m in range(HT):
                        ins = pe.matmul(banks[2 + u][0:rows, b * D:(b + 1) * D], hT[:, u, m, b * P:b * P + rows],
                                        w2_s[:, m, :], start=(m == 0), stop=(m == HT - 1))
                    if b == 0:
                        if not isinstance(c, int) or c > 0:
                            transpose_rows(0, c - 1, 1 - u, CHUNK)
                ins.then_inc(d["y"], 1)
            chunks(pe, mlp)
            transpose_rows(0, NCH, 0, REM)
            for a in range(1, 4):
                aggregate(a)

        @block.vector
        def _(dve):
            step = order(dve, s_setup)
            dve.wait_ge(s_const, 2)
            dve.tensor_scalar(before[:, :], iota[0:NG, 0:NG], iotap[0:NG, :], float(NWIN), ALU.is_gt, ALU.mult)
            dve.tensor_scalar(ident[:, :], iota[:, :], iotap[:, :], None, ALU.is_equal)
            dve.wait_ge(s_edge, 64)
            dve.tensor_copy(src_f, src_i)
            step(dve.tensor_copy(dst_f, dst_i))
            dve.tensor_reduce(gcol[:, 0:1], dst_f, AX_X, ALU.min)
            step(dve.scalar_tensor_tensor(out=mask_f, in0=dst_f, scalar=float(PAD_DST), in1=dst_f, op0=ALU.is_lt,
                                          op1=ALU.mult))
            step(dve.tensor_reduce(gcol[:, 1:2], mask_f, AX_X, ALU.max))
            dve.tensor_scalar(rel_f, dst_f, gcol[:, 0:1], None, ALU.subtract)
            dve.tensor_scalar(dst1_f, dst_f, 1.0, None, ALU.add)
            step(dve.tensor_tensor(gcol[:, 2:3], gcol[:, 1:2], gcol[:, 0:1], ALU.subtract))
            dve.tensor_scalar(gcol[:, 3:4], gcol[:, 2:3], float(WIN), None, ALU.is_ge).then_inc(s_edgef, 1)
            for n, t in enumerate((idx, rel, dst1)):
                for e in range(2):
                    dve.wait_ge(s_ptr, 2 * n + e + 1)
                    dve.tensor_copy(t[:, 0:NG, 4 * e:4 * e + 4].rearrange("p g t -> p t g"),
                                    banks[2 * n + e][:, :].rearrange("p (t g) -> p t g", g=P)[:, :, 0:NG]).then_inc(s_idx, 1)
            dve.wait_ge(s_ptr, 7)
            dve.tensor_copy(ctl[:, :, 0:3].rearrange("p g c -> p c g"),
                            banks[6][0:1, 0:3 * P].rearrange("p (c g) -> p c g", g=P)[:, :, 0:NG]).then_inc(s_idx, 1)

            dve.tensor_tensor(late[:, 0, :], least[:, :], banks[6][0:1, 0:NG], ALU.is_gt)
            dve.drain()
            dve.tensor_tensor(late[:, 1, :], late[:, 0, :], banks[6][0:1, P:P + NG], ALU.add)
            dve.drain()
            dve.tensor_reduce(late[:, 2, 0:1], late[:, 1, :], AX_X, ALU.max)
            dve.drain()
            dve.tensor_scalar(early[:, :], late[:, 2, 0:1], 0.5, None, ALU.is_lt).then_inc(s_idx, 1)
            dve.memset(acc[:, :, :], 0.0).then_inc(s_setup, 1)

            def one_hot(out, at, numbers):
                return dve.tensor_tensor(out, at.unsqueeze(2).to_broadcast([P, TILES, WIN]),
                                         numbers[:, :].unsqueeze(1).to_broadcast([P, TILES, WIN]), ALU.is_equal)

            def add(a, start, bank):
                if a == 0:
                    to = degrow[0:1, bass.ds(start, WIN)]
                    dve.tensor_tensor(to, to, bank[0:1, DH * WIN:DH * WIN + WIN], ALU.add)
                to = acc[:, :, bass.ds(start, WIN)]
                return dve.tensor_tensor(to, to, bank[:, 0:DH * WIN].rearrange("p (h n) -> p h n", h=DH), ALU.add)

            def hidden(c, u, n, i, done):
                dve.wait_ge(s_xt, c + 1)
                dve.wait_ge(aggs[0]["acc"], ACC0 + done)
                to = acc[:, :, cols(c, n)]
                dve.tensor_tensor(to, to, halves(banks[2 + u], n), ALU.add).then_inc(s_own, 1)
                for pr in range(HP):
                    dve.wait_ge(s_h, c * HP + pr + 1)
                    for e in range(2):
                        ins = dve.bn_stats(stats[:, 2 * pr + e, c, :], banks[pr % 2][:, e * CHUNK:e * CHUNK + n])
                    ins.then_inc(s_stats, 1)

            def aggregate(a):
                g = aggs[a]
                dve.sem_inc(g["acc"], ACC0)

                def hot_of(k, slot):
                    dve.wait_ge(g["sum"], SUM0 + k - 1)
                    one_hot(hot[:, slot, :, :], rel[:, k, :], iota).then_inc(g["hot"], 1)

                def group(k, q, i):
                    start = dve.value_load(ctl[0:1, k, 0:1], min_val=0, max_val=N - 1)
                    wide = dve.value_load(ctl[0:1, k, 1:2], min_val=0, max_val=1)
                    hot_of(k + 1, (q + 1) % 2)
                    wait_apart(dve, g["acc"], ACC0 + k)
                    with dve.If(wide > 0):
                        done = dve.value_load(ctl[0:1, k, 2:3], min_val=0, max_val=NWIN * NG)
                        dve.scalar_tensor_tensor(out=relx[:, 0, :], in0=rel[:, k, :], scalar=float(WIN),
                                                 in1=dst1[:, k, :], op0=ALU.is_ge, op1=ALU.mult)
                        dve.drain()
                        dve.tensor_scalar(relx[:, 1, :], relx[:, 0, :], float(WIN), None, ALU.add)
                        dve.drain()
                        with dve.Fori(0, NWIN) as w:
                            dve.tensor_scalar(relx[:, 1, :], relx[:, 1, :], -float(WIN), None, ALU.add)
                            dve.drain()
                            one_hot(hotx[:, :, :], relx[:, 1, :], iota1).then_inc(g["hotx"], 1)
                            dve.wait_ge(g["sumx"], done + w + 1)
                            add(a, w * WIN, banks[7]).then_inc(g["accx"], 1)
                            dve.wait_ge(g["accx"], done + w + 1)
                    dve.wait_ge(g["sum"], SUM0 + k + 1)
                    add(a, start, banks[5 + q % 2]).then_inc(g["acc"], 1)

                def retire(c, u, i, done):
                    if a == 0:
                        hidden(c, u, CHUNK, i, done)
                    else:
                        rows_done(a, c, u, CHUNK, i)

                def rest():
                    for chunk in LAST:
                        if a == 0:
                            hidden(*chunk, NG)
                        else:
                            rows_done(a, *chunk)
                hot_of(0, 0)
                passes(dve, group, retire, rest)

            def rows_done(a, c, u, n, i):
                d, K = dense[a], STEPS[a]
                rows, bs = min(n, P), blocks(n)
                nb = len(bs)
                r = slice(0, rows)
                bank = banks[2 + u][r, 0:nb * D].rearrange("p (b d) -> p b d", d=D)
                y = yt[r, 0:nb, :]
                at = [0]

                def step(*ins, apart=False):
                    at[0] += 1
                    ins[-1].then_inc(d["v"], 1)
                    (wait_apart if apart or at[0] == K else wait)(dve, d["v"], c * K + at[0])

                def scale(b):
                    return dinv[r, bass.ds(c * BPC + b, 1)]

                dve.wait_ge(d["y"], c + 1)
                if a == 0:
                    step(dve.tensor_tensor(y, bank, bias_bc[r, 0:1, :].to_broadcast([rows, nb, D]), ALU.add))
                else:
                    step(*[dve.scalar_tensor_tensor(out=yt[r, b, :], in0=bank[:, b, :], scalar=scale(b),
                                                    in1=bias_bc[r, a, :], op0=ALU.mult, op1=ALU.add) for b in range(nb)])
                if a in (1, 2):
                    wait(dve, d["st"][u], i * 16)
                    wait(dve, d["tt"], c - 1)
                    step(*[dve.tensor_scalar(ts[r, u, b, :], yt[r, b, :], 0.0, scale(b), ALU.max, ALU.mult)
                           for b in range(nb)])
                    return
                dve.wait_ge(d["xl"][u], i * 16 + 16)
                step(dve.scalar_tensor_tensor(out=y, in0=y, scalar=0.0, in1=xs[r, u, 0:nb, :], op0=ALU.max, op1=ALU.add))
                step(*[dve.bn_stats(lnst[r, b, :], yt[r, b, :]) for b in range(nb)], apart=True)
                step(*[dve.bn_aggr(lnmv[r, b, :], lnst[r, b, :]) for b in range(nb)])
                dve.wait_ge(d["std"], c + 1)
                step(dve.reciprocal(lnrec[r, 0:nb], lnstd[r, 0:nb]))
                wait(dve, d["st"][u], i * (32 if a == 0 else 16))
                step(*[dve.tensor_scalar(x1s[r, u, b, :], yt[r, b, :], lnmv[r, b, 0:1], lnrec[r, b:b + 1],
                                         ALU.subtract, ALU.mult) for b in range(nb)])
                if a == 0:
                    wait(dve, d["tt"], c - 1)
                    step(*[dve.tensor_scalar(ts[r, u, b, :], x1s[r, u, b, :], scale(b), None, ALU.mult)
                           for b in range(nb)])

            dve.wait_ge(s_setup, 5)
            dve.wait_ge(s_idx, 8)
            aggregate(0)

            step = order(dve, s_deg)
            dve.wait_ge(s_degt, 1)
            step(dve.tensor_scalar(degsum[:, :], banks[4][:, 0:NB], 1.0, None, ALU.add))
            dve.wait_ge(s_rt, 1)
            step(dve.reciprocal(dinv[:, :], degroot[:, :]))

            dve.wait_ge(s_stats, HP * (NCH + 1))
            for m in range(HT):
                ins = dve.bn_aggr(bnmv[:, m, :], stats[:, m, :, :].rearrange("p c s -> p (c s)"))
            step(ins)
            dve.wait_ge(s_wtc, 4)
            dve.wait_ge(s_rt, 2)
            b1_c, gamma_c, beta_c = (bncol[:, i * HT:(i + 1) * HT] for i in range(3))
            step(dve.reciprocal(bntmp[:, 1, :], bntmp[:, 0, :]))
            step(dve.tensor_tensor(bnscale[:, :], bntmp[:, 1, :], gamma_c, ALU.mult))
            step(dve.tensor_tensor(bntmp[:, 0, :], bnmv[:, :, 0], b1_c, ALU.add))
            step(dve.tensor_tensor(bntmp[:, 2, :], b1_c, bntmp[:, 0, :], ALU.subtract))
            step(dve.tensor_tensor(bntmp[:, 1, :], bntmp[:, 2, :], bnscale[:, :], ALU.mult))
            step(dve.tensor_tensor(bnbias[:, :], bntmp[:, 1, :], beta_c, ALU.add))

            chunks(dve, lambda c, u, n, i: rows_done(0, c, u, n, i))
            for a in range(1, 4):
                dve.wait_ge(dense[a - 1]["self"], NCH + 1)
                aggregate(a)


_INS = ['x', 'src', 'dst', 'L0_gnn_W1', 'L0_gnn_b1', 'L0_gnn_gamma', 'L0_gnn_beta', 'L0_gnn_W2', 'L0_gnn_b2',
        'L1_gnn_W1', 'L1_gnn_b1', 'L1_gnn_W2', 'L1_gnn_b2', 'L1_gnn_W3', 'L1_gnn_b3']


def kernel(**inputs):
    import numpy as _np
    import concourse.bacc as _bacc
    from concourse import mybir as _mybir
    from concourse.bass_utils import run_bass_kernel_spmd as _run

    nc = _bacc.Bacc("TRN2", target_bir_lowering=False, num_devices=1)
    arrays, t = {}, {}
    for name in _INS:
        a = _np.ascontiguousarray(inputs[name])
        arrays[f"in_{name}_dram"] = a
        t[name] = nc.dram_tensor(f"in_{name}_dram", a.shape, _mybir.dt.from_np(a.dtype), kind="ExternalInput").ap()
    out = nc.dram_tensor("out_0_dram", t["x"].shape, _mybir.dt.float32, kind="ExternalOutput").ap()
    gnn_kernel(nc, t["x"], t["src"], t["dst"], t["L0_gnn_W1"], t["L0_gnn_b1"], t["L0_gnn_gamma"], t["L0_gnn_beta"],
               t["L0_gnn_W2"], t["L0_gnn_b2"], [t[f"L1_gnn_W{i}"] for i in (1, 2, 3)],
               [t[f"L1_gnn_b{i}"] for i in (1, 2, 3)], out)
    r = _run(nc, [arrays], core_ids=[0])
    return r.results[0]["out_0_dram"]
```

```python
from contextlib import ExitStack

import concourse.bass as bass
from concourse import mybir

F32 = mybir.dt.float32
I32 = mybir.dt.int32
U32 = mybir.dt.uint32
ALU = mybir.AluOpType
ACT = mybir.ActivationFunctionType
AX_X = mybir.AxisListType.X

P = 128
TILES = 8
SLOTS = 4
LAG = 2
WIN = 128
CHUNK = 256
PAD_DST = 8192
EPS = 1e-5


def gnn_kernel(nc, x, src, dst, w1, b1, gamma, beta, w2, b2, wl, bl, out):
    N, D = x.shape
    E = src.shape[0]
    HID = w1.shape[1]
    DH, HT = D // P, HID // P
    GE = TILES * P
    NG = -(-E // GE)
    TAIL = E - (NG - 1) * GE
    NWIN = -(-N // WIN)
    NCOL = max(N, NWIN * WIN) + WIN
    NB = -(-N // P)
    NCH = N // CHUNK
    REM = N - NCH * CHUNK
    BPC = CHUNK // P
    NP = NG // (2 * SLOTS)
    assert NG % (2 * SLOTS) == 0 and NG <= P and NCH % 2 == 0 and 0 < REM <= P and D == 2 * P and HT % 2 == 0
    assert LAG == 2 and NCH == 2 * NP - LAG
    assert N < PAD_DST - WIN

    x1_d = nc.dram_tensor("x1_d", (N, D), F32).ap()
    tables = [nc.dram_tensor(f"table{i}_d", (N, D), F32).ap() for i in range(2)]
    h_d = nc.dram_tensor("h_d", ((NCH + 1) * P, HT * CHUNK), F32).ap()

    with ExitStack() as ctx:
        def sb(name, shape, dt=F32):
            return ctx.enter_context(nc.sbuf_tensor(name, shape, dt))

        def sem(name):
            return ctx.enter_context(nc.semaphore(name))

        banks = [ctx.enter_context(nc.psum_tensor(f"bank{i}", [P, 512], F32)) for i in range(8)]

        iota = sb("iota", [P, P])
        iota1 = sb("iota1", [P, P])
        iotap = sb("iotap", [P, 1])
        ident = sb("ident", [P, P])
        before = sb("before", [NG, NG])
        ones = sb("ones", [P, 1])
        zeros = sb("zeros", [P, DH])
        eps = sb("eps", [P, 1])
        w1_s = sb("w1_s", [P, DH, HID])
        w2_s = sb("w2_s", [P, HT, D])
        wt_s = sb("wt_s", [P, 3, DH, D])
        bnrow = sb("bnrow", [3 * HT, P])
        bncol = sb("bncol", [P, 3 * HT])
        bias_bc = sb("bias_bc", [P, 4, D])
        idx = sb("idx", [P, NG, TILES], I32)
        rel = sb("rel", [P, NG + 1, TILES])
        dst1 = sb("dst1", [P, NG, TILES])
        ctl = sb("ctl", [1, NG, 4], I32)
        early = sb("early", [1, 1], I32)
        least = sb("least", [1, NG + SLOTS])
        late = sb("late", [1, 3, NG])
        acc = sb("acc", [P, DH, NCOL])
        degrow = sb("degrow", [1, NCOL])
        ring = sb("ring", [P, SLOTS, TILES, D])
        idxbuf = sb("idxbuf", [P, SLOTS, TILES], I32)
        hot = sb("hot", [P, 2, TILES, WIN])
        hotx = sb("hotx", [P, TILES, WIN])
        hotsum = sb("hotsum", [P, 3, WIN])
        relx = sb("relx", [P, 2, TILES])
        deg = sb("deg", [NB, P])
        degsum = sb("degsum", [P, NB])
        degroot = sb("degroot", [P, NB])
        dinv = sb("dinv", [P, NB])
        stats = sb("stats", [P, HT, NCH + 1, 6])
        bnmv = sb("bnmv", [P, HT, 2])
        bntmp = sb("bntmp", [P, 3, HT])
        bnscale = sb("bnscale", [P, HT])
        bnbias = sb("bnbias", [P, HT])
        xs = sb("xs", [P, 2, BPC, D])
        x1s = sb("x1s", [P, 2, BPC, D])
        ts = sb("ts", [P, 2, BPC, D])
        hs = sb("hs", [P, 2, HT, CHUNK])
        us = sb("us", [P, 2, DH, CHUNK])
        yt = sb("yt", [P, BPC, D])
        lnst = sb("lnst", [P, BPC, 6])
        lnmv = sb("lnmv", [P, BPC, 2])
        lnstd = sb("lnstd", [P, BPC])
        lnrec = sb("lnrec", [P, BPC])

        spare = hs[0:NG, :, :, :].rearrange("p b m n -> p (b m n)")
        dst_i, src_i = spare[:, 0:GE].bitcast(I32), spare[:, GE:2 * GE].bitcast(I32)
        dst_f, src_f = spare[:, 2 * GE:3 * GE], spare[:, 3 * GE:4 * GE]
        rel_f, dst1_f = (t[0:NG, :, :, :].rearrange("p s b d -> p (s b d)") for t in (x1s, ts))
        mask_f = us[0:NG, :, :, :].rearrange("p s h n -> p (s h n)")
        gcol = sb("gcol", [NG, 6])
        ownrows = hs[:, :, :, :].rearrange("p u m n -> p u (m n)")[:, :, 0:BPC * D].rearrange(
            "p u (b d) -> p u b d", d=D)
        wraw = [hotx[:, i * 4:i * 4 + 4, :].rearrange("p t w -> p (t w)").rearrange("p (h d) -> p h d", h=DH)
                for i in range(2)] + [yt[:, :, :]]
        hT = ring[:, :, :, :].rearrange("p s t d -> p (s t d)")[:, 0:2 * HT * CHUNK].rearrange(
            "p (b m n) -> p b m n", b=2, m=HT)

        s_const = sem("s_const")
        s_edge = [sem(f"s_edge{i}") for i in range(2)]
        s_wts = sem("s_wts")
        s_setup = sem("s_setup")
        s_edgef = sem("s_edgef")
        s_ptr = sem("s_ptr")
        s_idx = sem("s_idx")
        s_wtp = sem("s_wtp")
        s_wtc = sem("s_wtc")
        s_h = sem("s_h")
        s_stats = sem("s_stats")
        s_hs = sem("s_hs")
        s_hst = [sem(f"s_hst{i}") for i in range(2)]
        s_hl = [sem(f"s_hl{i}") for i in range(2)]
        s_degl = sem("s_degl")
        s_degt = sem("s_degt")
        s_deg = sem("s_deg")
        s_rt = sem("s_rt")

        s_apart = sem("s_apart")

        aggs = [{
            "idxbuf": sem(f"s_idxbuf{a}"),
            "rows": [sem(f"s_rows{a}_{q}") for q in range(SLOTS)],
            "hot": sem(f"s_hot{a}"),
            "sum": sem(f"s_sum{a}"),
            "acc": sem(f"s_acc{a}"),
            "own": [sem(f"s_own{a}_{i}") for i in range(2)],
            "tt": sem(f"s_tt{a}"),
            "owned": sem(f"s_owned{a}"),
            "hotx": sem(f"s_hotx{a}"), "sumx": sem(f"s_sumx{a}"), "accx": sem(f"s_accx{a}"),
        } for a in range(4)]
        dense = [{
            "relu": sem(f"s_relu{a}"),
            "y": sem(f"s_y{a}"),
            "v": sem(f"s_v{a}"),
            "std": sem(f"s_std{a}"),
            "xl": [sem(f"s_dxl{a}_{i}") for i in range(2)],
            "st": [sem(f"s_st{a}_{i}") for i in range(2)],
            "zero": sem(f"s_zero{a}"),
        } for a in range(4)]
        STEPS = [7, 2, 2, 6]
        ADDED, NORMED = 2, 4
        HOTS = [2, 1, 1, 1]
        OWN = [2, 0, 0, 0]
        HP = HT // 2
        SUM0, ACC0 = SLOTS, 2

        block = ctx.enter_context(nc.Block())

        def wait(eng, s, n):
            if not isinstance(n, int) or n > 0:
                eng.wait_ge(s, n)

        def wait_apart(eng, s, n):
            wait(eng, s, n)
            if not isinstance(n, int):
                eng.sem_inc(s_apart)

        def order(eng, s, begun=0):
            n = [begun]

            def step(ins):
                n[0] += 1
                ins.then_inc(s, 1)
                eng.wait_ge(s, n[0])
            return step

        def if_early(eng, want):
            flag = eng.value_load(early[0:1, 0:1], min_val=0, max_val=1)
            return eng.If(flag > 0) if want else eng.If(flag < 1)

        def passes(eng, group, retire, ahead=0, between=None):
            def some(i, u, gs):
                for g in gs:
                    group(i * (2 * SLOTS) + ((u + ahead) * SLOTS + g), g, i * 2 + (u + ahead))

            def pair(i, last=False):
                for u in range(2):
                    more = not (last and ahead and u)
                    if more:
                        some(i, u, range(SLOTS - 1))
                    with if_early(eng, True):
                        retire(i * 2 + (u - LAG), u, i - LAG // 2, i * (2 * SLOTS) + ((u + 1) * SLOTS - 1))
                    if more:
                        some(i, u, range(SLOTS - 1, SLOTS))
            if ahead:
                some(0, -1, range(SLOTS))
            if between is not None:
                between()
            with eng.Fori(0, LAG) as r:
                for g in range(SLOTS):
                    group(r * SLOTS + (ahead * SLOTS + g), g, r + ahead)
            pair(1)
            with eng.Fori(2, NP - ahead) as i:
                pair(i)
            if ahead:
                pair(NP - 1, last=True)
            with if_early(eng, False):
                for u in range(2):
                    retire(u, u, 0, NG)
                with eng.Fori(1, NCH // 2) as i:
                    for u in range(2):
                        retire(i * 2 + u, u, i, NG)

        LAST = (NCH, 0, REM, NCH // 2)

        def chunks(eng, body):
            for u in range(2):
                body(u, u, CHUNK, 0)
            with eng.Fori(1, NCH // 2) as i:
                for u in range(2):
                    body(i * 2 + u, u, CHUNK, i)
            body(NCH, 0, REM, NCH // 2)

        def kept_first(eng, body, begun=False):
            if not begun:
                body(0, NCH, 0, REM, 0)
            body(1, NCH - 1, 1, CHUNK, 0)
            for u in range(2):
                body(2 + u, u, u, CHUNK, 1)
            with eng.Fori(2, NCH // 2) as i:
                for u in range(2):
                    body(i * 2 + u, i * 2 + (u - 2), u, CHUNK, i)
            body(NCH, NCH - 2, 0, CHUNK, NCH // 2)

        def step_chunk(s):
            if isinstance(s, int) and s < 2:
                return (NCH, REM) if s == 0 else (NCH - 1, CHUNK)
            return s - 2, CHUNK

        def relus(s):
            return range(HT) if isinstance(s, int) and s == 0 else (HT - 1,)

        def cols(c, n):
            return bass.ds(c * CHUNK, n)

        def blocks(n):
            return [(b, min(P, n - b * P)) for b in range(-(-n // P))]

        def rows_of(t, c, n):
            v = t[bass.ds(c * CHUNK, n), :]
            return v.rearrange("(b p) d -> p b d", p=P) if n == CHUNK else v

        def tile_of(buf, u, n):
            return buf[:, u, :, :] if n == CHUNK else buf[0:n, u, 0, :]

        def halves(bank, n):
            return bank[:, :].rearrange("p (h n) -> p h n", h=DH)[:, :, 0:n]

        def hidden_at(c):
            return h_d[bass.ds(c * P, P), :]

        def stored(eng, a, per):
            eng.wait_ge(dense[a]["st"][0], 16 * per * (NCH // 2 + 1))
            eng.wait_ge(dense[a]["st"][1], 16 * per * (NCH // 2))

        @block.sync
        def _(sp):
            sp.wait_ge(s_const, 1)
            at = (NG - 1) * GE
            for t, e, landed in ((src_i, src, s_edge[0]), (dst_i, dst, s_edge[1])):
                sp.dma_start(t[0:NG - 1, :], e[0:at].rearrange("(g e) -> g e", e=GE)).then_inc(landed, 16)
                sp.dma_start(t[NG - 1:NG, 0:TAIL], e[at:E].rearrange("(a e) -> a e", a=1)).then_inc(landed, 16)

            sp.dma_start(w1_s[:, :, :], w1.rearrange("(h p) n -> p h n", p=P)).then_inc(s_wts, 16)
            sp.dma_start(w2_s[:, :, :], w2.rearrange("(m p) n -> p m n", p=P)).then_inc(s_wts, 16)
            for l in range(3):
                sp.dma_start(wraw[l], wl[l].rearrange("(h p) n -> p h n", p=P)).then_inc(s_wts, 16)
            for i, v in enumerate((b1, gamma, beta)):
                sp.dma_start(bnrow[i * HT:(i + 1) * HT, :], v.rearrange("(m p) -> m p", p=P)).then_inc(s_wts, 16)
            for i, v in enumerate((b2, *bl)):
                sp.dma_start(bias_bc[:, i, :], v.rearrange("(a n) -> a n", a=1).to_broadcast([P, D])).then_inc(s_wts, 16)

            def load_own(a, c, u, n):
                wait(sp, aggs[a]["tt"], c - 1)
                sp.dma_start(tile_of(ownrows if a else xs, u, n),
                             rows_of((x, tables[0], tables[1], tables[0])[a], c, n)).then_inc(aggs[a]["own"][u], 16)

            def store_hidden(c, u):
                sp.wait_ge(s_hs, c * HP + HP)
                sp.dma_start(hidden_at(c), hs[:, u, :, :].rearrange("p m n -> p (m n)")).then_inc(s_hst[u], 16)

            def hidden_io(c, u, n, i):
                load_own(0, c, u, n)
                if not isinstance(c, int) or 0 < c < NCH:
                    store_hidden(c - 1, 1 - u)
            chunks(sp, hidden_io)

            sp.wait_ge(aggs[0]["acc"], ACC0 + NG)
            sp.wait_ge(s_const, 3)
            full = (NB - 1) * P
            sp.dma_start(deg[0:NB - 1, :], degrow[0:1, 0:full]).then_inc(s_degl, 16)
            sp.dma_start(deg[NB - 1:NB, 0:N - full], degrow[0:1, full:N]).then_inc(s_degl, 16)

            def dense_io(a, source, stores):
                d, K = dense[a], STEPS[a]

                def body(s, c, u, n, i):
                    if a > 0:
                        load_own(a, c, u, n)
                    if source is not None:
                        wait(sp, d["v"], (s - 2) * K + ADDED)
                        sp.dma_start(tile_of(xs, u, n), rows_of(source, c, n)).then_inc(d["xl"][u], 16)
                    if not isinstance(s, int) or s > 0:
                        store(s - 1, 1 - u)

                def store(s, u):
                    c, n = step_chunk(s) if a == 0 else (s, REM if isinstance(s, int) and s == NCH else CHUNK)
                    sp.wait_ge(d["v"], s * K + K)
                    for buf, t in stores:
                        sp.dma_start(rows_of(t, c, n), tile_of(buf, u, n)).then_inc(d["st"][u], 16)
                if a == 0:
                    kept_first(sp, body)
                else:
                    chunks(sp, lambda c, u, n, i: body(c, c, u, n, i))
                store(NCH, 0)

            sp.wait_ge(aggs[0]["tt"], NCH + 1)
            dense_io(0, x, ((x1s, x1_d), (ts, tables[0])))
            stored(sp, 0, 2)
            sp.wait_ge(dense[0]["relu"], NCH + HT)
            dense_io(1, None, ((ts, tables[1]),))
            stored(sp, 1, 1)
            dense_io(2, None, ((ts, tables[0]),))
            stored(sp, 2, 1)
            dense_io(3, x1_d, ((x1s, out),))
            stored(sp, 3, 1)

        @block.gpsimd
        def _(pool):
            first = TAIL // P * P
            pool.memset(src_i[:, first:GE], 0)
            pool.memset(dst_i[:, first:GE], PAD_DST).then_inc(s_const, 1)
            for t, base, step, cm in ((iota, 0, 1, 0), (iota1, 1, 1, 0), (iotap, 0, 0, 1)):
                pool.iota(t[:, :], pattern=[[step, t.shape[1]]], base=base, channel_multiplier=cm,
                          allow_small_or_imprecise_dtypes=True)
            pool.iota(least[:, :], pattern=[[CHUNK, NG // SLOTS + 1], [0, SLOTS]], base=-LAG * CHUNK,
                      channel_multiplier=0, allow_small_or_imprecise_dtypes=True)
            pool.memset(rel[:, NG, :], float(PAD_DST))
            pool.memset(ones[:, :], 1.0)
            pool.memset(zeros[:, :], 0.0)
            pool.memset(eps[:, :], EPS).then_inc(s_const, 1)
            pool.memset(degrow[:, :], 0.0)
            pool.memset(deg[:, :], 0.0).then_inc(s_const, 1)

            def gather(a, table):
                g = aggs[a]

                with pool.Fori(0, NG // SLOTS) as i:
                    for q in range(SLOTS):
                        k = i * SLOTS + q
                        pool.wait_ge(g["sum"], SUM0 + k + 1 - SLOTS)
                        wait_apart(pool, g["idxbuf"], k + 1)
                        for j in range(TILES):
                            at = bass.IndirectOffsetOnAxis(ap=idxbuf[:, q, j:j + 1].bitcast(U32), axis=0)
                            pool.indirect_dma_start(out=ring[:, q, j, :], out_offset=None, in_=table[:, :],
                                                    in_offset=at).then_inc(g["rows"][q], 16)

            gather(0, x)
            pool.wait_ge(s_hst[0], 16 * (NCH // 2))
            pool.wait_ge(s_hst[1], 16 * (NCH // 2 - 1))

            def load_hidden(s, c, u, n, i):
                if not isinstance(s, int) or s > 1:
                    pool.wait_ge(dense[0]["relu"], s + (HT - 2))
                    pool.dma_start(hs[:, u, :, :].rearrange("p m n -> p (m n)"), hidden_at(c)).then_inc(s_hl[u], 16)
            kept_first(pool, load_hidden)
            stored(pool, 0, 2)
            gather(1, tables[0])
            stored(pool, 1, 1)
            gather(2, tables[1])
            stored(pool, 2, 1)
            gather(3, tables[0])

        @block.scalar
        def _(act):
            def roots(a, s, n):
                d = dense[a]
                rows, nb = min(n, P), len(blocks(n))
                act.wait_ge(d["v"], s * STEPS[a] + NORMED)
                act.activation(lnstd[0:rows, 0:nb], lnmv[0:rows, 0:nb, 1], ACT.Sqrt,
                               bias=eps[0:rows, :]).then_inc(d["std"], 1)

            def keep_hidden(c, u, n, i):
                wait(act, s_hst[u], i * 16)
                for pr in range(HP):
                    act.wait_ge(s_stats, c * HP + pr + 1)
                    act.copy(hs[:, u, 2 * pr:2 * pr + 2, 0:n],
                             banks[pr % 2][:, :].rearrange("p (e n) -> p e n", e=2)[:, :, 0:n]).then_inc(s_hs, 1)

            def aggregate(a, between=None):
                g = aggs[a]

                def group(k, q, i):
                    if isinstance(i, int) and i == 0 and a > 0:
                        act.wait_ge(aggs[a - 1]["rows"][q], NG // SLOTS * (16 * TILES))
                    wait(act, g["rows"][q], i * (16 * TILES))
                    act.copy(idxbuf[:, q, :], idx[:, k, :]).then_inc(g["idxbuf"], 1)

                def retire(c, u, i, need, n=CHUNK):
                    if a == 0:
                        keep_hidden(c, u, n, i)
                    elif a == 3:
                        roots(a, c, n)
                passes(act, group, retire, ahead=1, between=between)
                retire(*LAST[0:2], LAST[3], NG, REM)

            def weights():
                for l in range(3):
                    act.wait_ge(s_wtp, l + 1)
                    act.copy(wt_s[:, l, :, :], halves(banks[2 + l], D)).then_inc(s_wtc, 1)
                act.wait_ge(s_wtp, 4)
                act.copy(bncol[:, :], banks[7][:, 0:3 * HT]).then_inc(s_wtc, 1)
                act.wait_ge(s_idx, 8)

            act.wait_ge(s_idx, 2)
            aggregate(0, weights)
            act.wait_ge(s_deg, 1)
            act.activation(bntmp[:, 0, :], bnmv[:, :, 1], ACT.Sqrt, bias=eps[:, :]).then_inc(s_rt, 1)
            act.wait_ge(s_deg, 7)

            def mlp(s, c, u, n, i):
                d = dense[0]
                wait(act, s_hl[u], i * 16)
                wait(act, d["y"], s - 1)
                for m in range(HT):
                    ins = act.activation(hT[:, u, m, 0:n], hs[:, u, m, 0:n], ACT.Relu,
                                         scale=bnscale[:, m:m + 1], bias=bnbias[:, m:m + 1])
                    if m in relus(s):
                        ins.then_inc(d["relu"], 1)
                if not isinstance(s, int) or s > 0:
                    roots(0, s - 1, step_chunk(s - 1)[1])
            mlp(0, NCH, 0, REM, 0)
            act.wait_ge(s_deg, 8)
            act.activation(degroot[:, :], degsum[:, :], ACT.Sqrt).then_inc(s_rt, 1)
            kept_first(act, mlp, begun=True)
            roots(0, NCH, CHUNK)
            for a in range(1, 4):
                aggregate(a)

        @block.tensor
        def _(pe):
            for g in aggs:
                pe.sem_inc(g["sum"], SUM0)
            for i, t in enumerate((src_f, rel_f, dst1_f)):
                pe.wait_ge(s_edgef, 1 + (i > 0))
                for j in range(TILES):
                    ins = pe.transpose(banks[2 * i + j // 4][:, (j % 4) * P:(j % 4) * P + NG],
                                       t[:, j * P:(j + 1) * P], ident[0:NG, 0:NG])
                    if j % 4 == 3:
                        ins.then_inc(s_ptr, 1)
            pe.matmul(banks[6][0:1, 0:NG], gcol[:, 0:1], ident[0:NG, 0:NG], start=True, stop=True)
            pe.matmul(banks[6][0:1, P:P + NG], gcol[:, 3:4], ident[0:NG, 0:NG], start=True, stop=True)
            pe.matmul(banks[6][0:1, 2 * P:2 * P + NG], gcol[:, 3:4], before[:, :], start=True,
                      stop=True).then_inc(s_ptr, 1)

            pe.wait_ge(s_idx, 8)

            pe.wait_ge(s_wts, 16 * 12)
            for l in range(3):
                for ih in range(DH):
                    for oh in range(DH):
                        at = ih * D + oh * P
                        ins = pe.transpose(banks[2 + l][:, at:at + P], wraw[l][:, oh, ih * P:(ih + 1) * P],
                                           ident[:, :])
                ins.then_inc(s_wtp, 1)
            pe.transpose(banks[7][:, 0:3 * HT], bnrow[:, :], ident[0:3 * HT, 0:3 * HT]).then_inc(s_wtp, 1)
            pe.wait_ge(s_wtc, 4)

            def sums(a, bank, rows, hots, total, signal):
                if a == 0:
                    pe.matmul(bank[0:1, DH * WIN:DH * WIN + WIN], ones[:, :], total, start=True, stop=True)
                for h in range(DH):
                    for j in range(TILES):
                        ins = pe.matmul(bank[:, h * WIN:(h + 1) * WIN], rows[:, j, h * P:(h + 1) * P], hots[:, j, :],
                                        start=(j == 0), stop=(j == TILES - 1))
                ins.then_inc(signal, 1)

            def transpose_own(a, c, u, n, i):
                g = aggs[a]
                pe.wait_ge(g["own"][u], i * 16 + 16)
                wait(pe, g["owned"], c - 1)
                for b, rows in blocks(n):
                    for h in range(DH):
                        at = h * CHUNK + b * P
                        ins = pe.transpose(banks[OWN[a] + u][:, at:at + rows],
                                           (ownrows if a else xs)[0:rows, u, b, h * P:(h + 1) * P],
                                           ident[0:rows, 0:rows])
                ins.then_inc(g["tt"], 1)

            def hidden(c, u, n, i):
                transpose_own(0, c, u, n, i)
                pe.wait_ge(aggs[0]["owned"], c + 1)
                for pr in range(HP):
                    wait(pe, s_hs, c * HP + pr - 1)
                    for e in range(2):
                        m = 2 * pr + e
                        for h in range(DH):
                            ins = pe.matmul(banks[pr % 2][:, e * CHUNK:e * CHUNK + n], w1_s[:, h, m * P:(m + 1) * P],
                                            acc[:, h, cols(c, n)], start=(h == 0), stop=(h == DH - 1))
                    ins.then_inc(s_h, 1)

            def layer(a, c, u, n):
                d = dense[a]
                pe.wait_ge(aggs[a]["owned"], c + 1)
                wait(pe, d["v"], (c - 2) * STEPS[a] + 1)
                for b, rows in blocks(n):
                    for h in range(DH):
                        ins = pe.matmul(banks[2 + u][0:rows, b * D:(b + 1) * D], us[:, u, h, b * P:b * P + rows],
                                        wt_s[:, a - 1, h, :], start=(h == 0), stop=(h == DH - 1))
                ins.then_inc(d["y"], 1)

            def aggregate(a):
                g = aggs[a]

                def group(k, q, i):
                    wide = pe.value_load(ctl[0:1, k, 1:2], min_val=0, max_val=1)
                    pe.wait_ge(g["hot"], (k + 1) * HOTS[a])
                    pe.wait_ge(g["rows"][q], i * (16 * TILES) + 16 * TILES)
                    with pe.If(wide > 0):
                        done = pe.value_load(ctl[0:1, k, 2:3], min_val=0, max_val=NWIN * NG)
                        with pe.Fori(0, NWIN) as w:
                            pe.wait_ge(g["hotx"], (done + w) * HOTS[a] + HOTS[a])
                            sums(a, banks[7], ring[:, q, :, :], hotx, hotsum[:, 2, :], g["sumx"])
                    pe.wait_ge(g["acc"], ACC0 + k - 1)
                    sums(a, banks[5 + q % 2], ring[:, q, :, :], hot[:, q % 2, :, :],
                         hotsum[:, q % 2, :], g["sum"])

                def retire(c, u, i, done, n=CHUNK):
                    if a == 0:
                        hidden(c, u, n, i)
                    else:
                        transpose_own(a, c, u, n, i)
                        layer(a, c, u, n)
                passes(pe, group, retire)
                retire(*LAST[0:2], LAST[3], NG, REM)

            aggregate(0)
            pe.wait_ge(s_degl, 32)
            pe.transpose(banks[4][:, 0:NB], deg[:, :], ident[0:NB, 0:NB]).then_inc(s_degt, 1)

            def mlp(s, c, u, n, i):
                d = dense[0]
                wait(pe, d["v"], (s - 2) * STEPS[0] + 1)
                first = isinstance(s, int) and s == 0
                for b, rows in blocks(n):
                    for m in range(HT):
                        if b == 0 and (first or m == 0):
                            pe.wait_ge(d["relu"], m + 1 if first else s + HT)
                        ins = pe.matmul(banks[2 + u][0:rows, b * D:(b + 1) * D], hT[:, u, m, b * P:b * P + rows],
                                        w2_s[:, m, :], start=(m == 0), stop=(m == HT - 1))
                ins.then_inc(d["y"], 1)
            kept_first(pe, mlp)
            for a in range(1, 4):
                aggregate(a)

        @block.vector
        def _(dve):
            step = order(dve, s_setup)
            dve.wait_ge(s_const, 2)
            dve.tensor_scalar(ident[:, :], iota[:, :], iotap[:, :], None, ALU.is_equal)
            dve.tensor_scalar(before[:, :], iota[0:NG, 0:NG], iotap[0:NG, :], float(NWIN), ALU.is_gt, ALU.mult)
            dve.wait_ge(s_edge[0], 32)
            dve.tensor_copy(src_f, src_i).then_inc(s_edgef, 1)
            dve.wait_ge(s_edge[1], 32)
            step(dve.tensor_copy(dst_f, dst_i))

            def by_edge(n, t):
                for e in range(2):
                    dve.wait_ge(s_ptr, 2 * n + e + 1)
                    dve.tensor_copy(t[:, 0:NG, 4 * e:4 * e + 4].rearrange("p g t -> p t g"),
                                    banks[2 * n + e][:, :].rearrange("p (t g) -> p t g", g=P)[:, :, 0:NG]).then_inc(s_idx, 1)
            by_edge(0, idx)
            dve.tensor_reduce(gcol[:, 0:1], dst_f, AX_X, ALU.min)
            step(dve.scalar_tensor_tensor(out=mask_f, in0=dst_f, scalar=float(PAD_DST), in1=dst_f, op0=ALU.is_lt,
                                          op1=ALU.mult))
            step(dve.tensor_reduce(gcol[:, 1:2], mask_f, AX_X, ALU.max))
            dve.tensor_scalar(rel_f, dst_f, gcol[:, 0:1], None, ALU.subtract)
            dve.tensor_scalar(dst1_f, dst_f, 1.0, None, ALU.add)
            step(dve.tensor_tensor(gcol[:, 2:3], gcol[:, 1:2], gcol[:, 0:1], ALU.subtract))
            dve.tensor_scalar(gcol[:, 3:4], gcol[:, 2:3], float(WIN), None, ALU.is_ge).then_inc(s_edgef, 1)
            by_edge(1, rel)
            by_edge(2, dst1)
            dve.wait_ge(s_ptr, 7)
            dve.tensor_copy(ctl[:, :, 0:3].rearrange("p g c -> p c g"),
                            banks[6][0:1, 0:3 * P].rearrange("p (c g) -> p c g", g=P)[:, :, 0:NG]).then_inc(s_idx, 1)

            dve.tensor_tensor(late[:, 0, :], least[:, 1:NG + 1], banks[6][0:1, 0:NG], ALU.is_gt)
            dve.drain()
            dve.tensor_tensor(late[:, 1, :], late[:, 0, :], banks[6][0:1, P:P + NG], ALU.add)
            dve.drain()
            dve.tensor_reduce(late[:, 2, 0:1], late[:, 1, :], AX_X, ALU.max)
            dve.drain()
            dve.tensor_scalar(early[:, :], late[:, 2, 0:1], 0.5, None, ALU.is_lt).then_inc(s_idx, 1)

            def one_hot(a, out, at, numbers, total, signal, n):
                dve.tensor_tensor(out, at.unsqueeze(2).to_broadcast([P, TILES, WIN]),
                                  numbers[:, :].unsqueeze(1).to_broadcast([P, TILES, WIN]), ALU.is_equal).then_inc(signal, 1)
                if a == 0:
                    dve.wait_ge(signal, n * HOTS[0] + 1)
                    dve.tensor_reduce(total, out.rearrange("p t w -> p w t"), AX_X, ALU.add).then_inc(signal, 1)

            def add(a, start, bank):
                if a == 0:
                    to = degrow[0:1, bass.ds(start, WIN)]
                    dve.tensor_tensor(to, to, bank[0:1, DH * WIN:DH * WIN + WIN], ALU.add)
                to = acc[:, :, bass.ds(start, WIN)]
                return dve.tensor_tensor(to, to, bank[:, 0:DH * WIN].rearrange("p (h n) -> p h n", h=DH), ALU.add)

            def hidden(c, u, n, i, done):
                dve.wait_ge(aggs[0]["tt"], c + 1)
                dve.wait_ge(aggs[0]["acc"], ACC0 + done)
                to = acc[:, :, cols(c, n)]
                dve.tensor_tensor(to, to, halves(banks[OWN[0] + u], n), ALU.add).then_inc(aggs[0]["owned"], 1)
                for pr in range(HP):
                    dve.wait_ge(s_h, c * HP + pr + 1)
                    for e in range(2):
                        ins = dve.bn_stats(stats[:, 2 * pr + e, c, :], banks[pr % 2][:, e * CHUNK:e * CHUNK + n])
                    ins.then_inc(s_stats, 1)
                    if isinstance(c, int) and c == NCH:
                        dve.wait_ge(s_stats, c * HP + pr + 1)
                        for m in range(2 * pr, 2 * pr + 2):
                            ins = dve.bn_aggr(bnmv[:, m, :], stats[:, m, :, :].rearrange("p c s -> p (c s)"))
                        if pr == HP - 1:
                            ins.then_inc(s_deg, 1)

            def take(a, c, u, n, done):
                g = aggs[a]
                dve.wait_ge(g["tt"], c + 1)
                wait(dve, dense[a]["y"], c - 1)
                dve.wait_ge(g["acc"], ACC0 + done)
                dve.tensor_tensor(us[:, u, :, 0:n], acc[:, :, cols(c, n)], halves(banks[OWN[a] + u], n),
                                  ALU.add).then_inc(g["owned"], 1)

            def empty(a, c, n):
                zero = zeros[:, :].unsqueeze(2).to_broadcast([P, DH, n])
                dve.tensor_copy(acc[:, :, cols(c, n)], zero).then_inc(dense[a]["zero"], 1)

            def aggregate(a):
                g = aggs[a]
                dve.sem_inc(g["acc"], ACC0)

                def hot_of(k, slot):
                    dve.wait_ge(g["sum"], SUM0 + k - 1)
                    one_hot(a, hot[:, slot, :, :], rel[:, k, :], iota, hotsum[:, slot, :], g["hot"], k)

                def group(k, q, i):
                    start = dve.value_load(ctl[0:1, k, 0:1], min_val=0, max_val=N - 1)
                    wide = dve.value_load(ctl[0:1, k, 1:2], min_val=0, max_val=1)
                    hot_of(k + 1, (q + 1) % 2)
                    wait_apart(dve, g["acc"], ACC0 + k)
                    with dve.If(wide > 0):
                        done = dve.value_load(ctl[0:1, k, 2:3], min_val=0, max_val=NWIN * NG)
                        dve.scalar_tensor_tensor(out=relx[:, 0, :], in0=rel[:, k, :], scalar=float(WIN),
                                                 in1=dst1[:, k, :], op0=ALU.is_ge, op1=ALU.mult)
                        dve.drain()
                        dve.tensor_scalar(relx[:, 1, :], relx[:, 0, :], float(WIN), None, ALU.add)
                        dve.drain()
                        with dve.Fori(0, NWIN) as w:
                            dve.tensor_scalar(relx[:, 1, :], relx[:, 1, :], -float(WIN), None, ALU.add)
                            dve.drain()
                            one_hot(a, hotx[:, :, :], relx[:, 1, :], iota1, hotsum[:, 2, :], g["hotx"], done + w)
                            dve.wait_ge(g["sumx"], done + w + 1)
                            add(a, w * WIN, banks[7]).then_inc(g["accx"], 1)
                            dve.wait_ge(g["accx"], done + w + 1)
                    dve.wait_ge(g["sum"], SUM0 + k + 1)
                    add(a, start, banks[5 + q % 2]).then_inc(g["acc"], 1)

                def retire(c, u, i, done, n=CHUNK):
                    if a == 0:
                        hidden(c, u, n, i, done)
                    else:
                        take(a, c, u, n, done)
                        rows_done(a, c, c, u, n, i)
                        if a < 3:
                            empty(a, c, n)
                hot_of(0, 0)
                if a == 0:
                    dve.memset(acc[:, :, :], 0.0).then_inc(s_setup, 1)
                    dve.wait_ge(s_setup, 5)
                passes(dve, group, retire)
                retire(*LAST[0:2], LAST[3], NG, REM)

            def rows_done(a, s, c, u, n, i):
                d, K = dense[a], STEPS[a]
                rows, bs = min(n, P), blocks(n)
                nb = len(bs)
                r = slice(0, rows)
                bank = banks[2 + u][r, 0:nb * D].rearrange("p (b d) -> p b d", d=D)
                y = yt[r, 0:nb, :]
                at = [0]

                def step(*ins, apart=False):
                    at[0] += 1
                    ins[-1].then_inc(d["v"], 1)
                    (wait_apart if apart or at[0] == K else wait)(dve, d["v"], s * K + at[0])

                def scale(b):
                    return dinv[r, bass.ds(c * BPC + b, 1)]

                dve.wait_ge(d["y"], s + 1)
                if a == 0:
                    step(dve.tensor_tensor(y, bank, bias_bc[r, 0:1, :].to_broadcast([rows, nb, D]), ALU.add))
                else:
                    step(*[dve.scalar_tensor_tensor(out=yt[r, b, :], in0=bank[:, b, :], scalar=scale(b),
                                                    in1=bias_bc[r, a, :], op0=ALU.mult, op1=ALU.add) for b in range(nb)])
                if a in (1, 2):
                    wait(dve, d["st"][u], i * 16)
                    step(*[dve.tensor_scalar(ts[r, u, b, :], yt[r, b, :], 0.0, scale(b), ALU.max, ALU.mult)
                           for b in range(nb)])
                    return
                dve.wait_ge(d["xl"][u], i * 16 + 16)
                step(dve.scalar_tensor_tensor(out=y, in0=y, scalar=0.0, in1=xs[r, u, 0:nb, :], op0=ALU.max, op1=ALU.add))
                step(*[dve.bn_stats(lnst[r, b, :], yt[r, b, :]) for b in range(nb)], apart=True)
                step(*[dve.bn_aggr(lnmv[r, b, :], lnst[r, b, :]) for b in range(nb)])
                dve.wait_ge(d["std"], s + 1)
                step(dve.reciprocal(lnrec[r, 0:nb], lnstd[r, 0:nb]))
                wait(dve, d["st"][u], i * (32 if a == 0 else 16))
                step(*[dve.tensor_scalar(x1s[r, u, b, :], yt[r, b, :], lnmv[r, b, 0:1], lnrec[r, b:b + 1],
                                         ALU.subtract, ALU.mult) for b in range(nb)])
                if a == 0:
                    step(*[dve.tensor_scalar(ts[r, u, b, :], x1s[r, u, b, :], scale(b), None, ALU.mult)
                           for b in range(nb)])
                    empty(a, c, n)

            dve.wait_ge(s_const, 3)
            dve.wait_ge(s_idx, 8)
            dve.wait_ge(s_wtp, 3)
            aggregate(0)

            step = order(dve, s_deg, 1)
            dve.wait_ge(s_wtc, 4)
            dve.wait_ge(s_rt, 1)
            b1_c, gamma_c, beta_c = (bncol[:, i * HT:(i + 1) * HT] for i in range(3))
            step(dve.reciprocal(bntmp[:, 1, :], bntmp[:, 0, :]))
            step(dve.tensor_tensor(bnscale[:, :], bntmp[:, 1, :], gamma_c, ALU.mult))
            step(dve.tensor_tensor(bntmp[:, 0, :], bnmv[:, :, 0], b1_c, ALU.add))
            step(dve.tensor_tensor(bntmp[:, 2, :], b1_c, bntmp[:, 0, :], ALU.subtract))
            step(dve.tensor_tensor(bntmp[:, 1, :], bntmp[:, 2, :], bnscale[:, :], ALU.mult))
            step(dve.tensor_tensor(bnbias[:, :], bntmp[:, 1, :], beta_c, ALU.add))

            dve.wait_ge(s_degt, 1)
            step(dve.tensor_scalar(degsum[:, :], banks[4][:, 0:NB], 1.0, None, ALU.add))
            dve.wait_ge(s_rt, 2)
            step(dve.reciprocal(dinv[:, :], degroot[:, :]))

            kept_first(dve, lambda s, c, u, n, i: rows_done(0, s, c, u, n, i))
            for a in range(1, 4):
                dve.wait_ge(dense[a - 1]["zero"], NCH + 1)
                aggregate(a)


_INS = ['x', 'src', 'dst', 'L0_gnn_W1', 'L0_gnn_b1', 'L0_gnn_gamma', 'L0_gnn_beta', 'L0_gnn_W2', 'L0_gnn_b2',
        'L1_gnn_W1', 'L1_gnn_b1', 'L1_gnn_W2', 'L1_gnn_b2', 'L1_gnn_W3', 'L1_gnn_b3']


def kernel(**inputs):
    import numpy as _np
    import concourse.bacc as _bacc
    from concourse import mybir as _mybir
    from concourse.bass_utils import run_bass_kernel_spmd as _run

    nc = _bacc.Bacc("TRN2", target_bir_lowering=False, num_devices=1)
    arrays, t = {}, {}
    for name in _INS:
        a = _np.ascontiguousarray(inputs[name])
        arrays[f"in_{name}_dram"] = a
        t[name] = nc.dram_tensor(f"in_{name}_dram", a.shape, _mybir.dt.from_np(a.dtype), kind="ExternalInput").ap()
    out = nc.dram_tensor("out_0_dram", t["x"].shape, _mybir.dt.float32, kind="ExternalOutput").ap()
    gnn_kernel(nc, t["x"], t["src"], t["dst"], t["L0_gnn_W1"], t["L0_gnn_b1"], t["L0_gnn_gamma"], t["L0_gnn_beta"],
               t["L0_gnn_W2"], t["L0_gnn_b2"], [t[f"L1_gnn_W{i}"] for i in (1, 2, 3)],
               [t[f"L1_gnn_b{i}"] for i in (1, 2, 3)], out)
    r = _run(nc, [arrays], core_ids=[0])
    return r.results[0]["out_0_dram"]
```
